# Optimizing a Trainium2 kernel written in Bass

```python
import numpy as np
import jax
import jax.numpy as jnp

def _softmax(x, axis=-1):
    return jax.nn.softmax(x, axis=axis)

def _gelu(x):
    return jax.nn.gelu(x, approximate=True)

def _silu(x):
    return jax.nn.silu(x)

def _sigmoid(x):
    return jax.nn.sigmoid(x)

def _layernorm(x, axis=-1, eps=1e-05):
    m = jnp.mean(x, axis=axis, keepdims=True)
    v = jnp.var(x, axis=axis, keepdims=True)
    return (x - m) / jnp.sqrt(v + eps)

def _scatter_add(tgt, idx, src, axis=0):
    return tgt.at[idx].add(src)

def _segment_sum(src, seg, n):
    return jax.ops.segment_sum(src, seg, n)
kernel_name = 'mk_seq_postln_d1_jaxref_r8_28b925'

def setup_inputs(seed: int=0):
    np.random.seed(seed)
    _w = jnp.asarray

    def _L0_attn_setup():
        import math
        import jax, jax.numpy as jnp
        import numpy as np
        B, T, C, H = (8, 128, 128, 16)
        HD = C // H
        key = jax.random.key(seed)
        ks = jax.random.split(key, 7)
        return {'x': jax.random.normal(ks[0], (B, T, C), dtype=jnp.float32), 'Wattn': jax.random.normal(ks[1], (C, 3 * C), dtype=jnp.float32) * 0.02, 'battn': jax.random.normal(ks[2], (3 * C,), dtype=jnp.float32) * 0.02, 'Wproj': jax.random.normal(ks[3], (C, C), dtype=jnp.float32) * 0.02, 'bproj': jax.random.normal(ks[4], (C,), dtype=jnp.float32) * 0.02, 'embk': jax.random.normal(ks[5], (T, HD), dtype=jnp.float32) * 0.02, 'embv': jax.random.normal(ks[6], (T, HD), dtype=jnp.float32) * 0.02}
    _L0_attn_in = _L0_attn_setup()

    def _L0_ffn_setup():
        import jax, jax.numpy as jnp
        import numpy as np
        B, S, H, I, E_ROUTED, TOP_K = (8, 256, 128, 256, 8, 2)

        def _expert(x, Wg, Wu, Wd):
            return jax.nn.silu(x @ Wg.T) * (x @ Wu.T) @ Wd.T
        key = jax.random.key(seed)
        ks = jax.random.split(key, 9)
        s = 0.02
        return {'x': jax.random.normal(ks[0], (B, S, H), dtype=jnp.float32), 'Wg_s': jax.random.normal(ks[1], (I, H), dtype=jnp.float32) * s, 'Wu_s': jax.random.normal(ks[2], (I, H), dtype=jnp.float32) * s, 'Wd_s': jax.random.normal(ks[3], (H, I), dtype=jnp.float32) * s, 'Wg': jax.random.normal(ks[4], (E_ROUTED, I, H), dtype=jnp.float32) * s, 'Wu': jax.random.normal(ks[5], (E_ROUTED, I, H), dtype=jnp.float32) * s, 'Wd': jax.random.normal(ks[6], (E_ROUTED, H, I), dtype=jnp.float32) * s, 'Wr': jax.random.normal(ks[7], (E_ROUTED, H), dtype=jnp.float32) * s, 'rb': jnp.zeros((E_ROUTED,), dtype=jnp.float32)}
    _L0_ffn_in = _L0_ffn_setup()
    _d = {'L0_attn_x': _L0_attn_in['x'], 'L0_attn_Wattn': _L0_attn_in['Wattn'], 'L0_attn_battn': _L0_attn_in['battn'], 'L0_attn_Wproj': _L0_attn_in['Wproj'], 'L0_attn_bproj': _L0_attn_in['bproj'], 'L0_attn_embk': _L0_attn_in['embk'], 'L0_attn_embv': _L0_attn_in['embv'], 'L0_ffn_Wg_s': _L0_ffn_in['Wg_s'], 'L0_ffn_Wu_s': _L0_ffn_in['Wu_s'], 'L0_ffn_Wd_s': _L0_ffn_in['Wd_s'], 'L0_ffn_Wg': _L0_ffn_in['Wg'], 'L0_ffn_Wu': _L0_ffn_in['Wu'], 'L0_ffn_Wd': _L0_ffn_in['Wd'], 'L0_ffn_Wr': _L0_ffn_in['Wr'], 'L0_ffn_rb': _L0_ffn_in['rb']}
    _x0 = _d['L0_attn_x']
    _d['L0_attn_x'] = jax.random.normal(jax.random.fold_in(jax.random.key(seed), 1), (16, 256, 128), dtype=_x0.dtype)
    del _x0
    return _d

def reference(L0_attn_x, L0_attn_Wattn, L0_attn_battn, L0_attn_Wproj, L0_attn_bproj, L0_attn_embk, L0_attn_embv, L0_ffn_Wg_s, L0_ffn_Wu_s, L0_ffn_Wd_s, L0_ffn_Wg, L0_ffn_Wu, L0_ffn_Wd, L0_ffn_Wr, L0_ffn_rb):

    def _L0_attn_ref(x, Wattn, battn, Wproj, bproj, embk, embv):
        import math
        import jax, jax.numpy as jnp
        import numpy as np
        B, T, C, H = (8, 128, 128, 16)
        HD = C // H
        b, t, c = x.shape
        qkv = x @ Wattn + battn
        q, k, v = jnp.split(qkv, 3, axis=-1)
        q = q.reshape(b, t, H, HD).transpose(0, 2, 1, 3)
        k = k.reshape(b, t, H, HD).transpose(0, 2, 1, 3)
        v = v.reshape(b, t, H, HD).transpose(0, 2, 1, 3)
        idx = jnp.arange(t)
        rel = jnp.tril(idx[:, None] - idx[None, :])
        rk = embk[rel]
        rv = embv[rel]
        scale = 1.0 / math.sqrt(HD)
        att1 = jnp.einsum('bhtd,bhsd->bhts', q, k) * scale
        att2 = jnp.einsum('bhtd,tsd->bhts', q, rk)
        att = att1 + att2
        causal = idx[None, :] <= idx[:, None]
        att = jnp.where(causal[None, None], att, -jnp.inf)
        att = jax.nn.softmax(att, axis=-1)
        y1 = jnp.einsum('bhts,bhsd->bhtd', att, v)
        y2 = jnp.einsum('bhts,tsd->bhtd', att, rv)
        y = (y1 + y2).transpose(0, 2, 1, 3).reshape(b, t, c)
        return y @ Wproj + bproj

    def _L0_ffn_ref(x, Wg_s, Wu_s, Wd_s, Wg, Wu, Wd, Wr, rb):
        import jax, jax.numpy as jnp
        import numpy as np
        B, S, H, I, E_ROUTED, TOP_K = (8, 256, 128, 256, 8, 2)

        def _expert(x, Wg, Wu, Wd):
            return jax.nn.silu(x @ Wg.T) * (x @ Wu.T) @ Wd.T
        shared = _expert(x, Wg_s, Wu_s, Wd_s)
        logits = jnp.einsum('bsh,eh->bse', x, Wr) + rb
        probs = jax.nn.sigmoid(logits)
        scores, idx = jax.lax.top_k(probs, TOP_K)
        cw = (jax.nn.one_hot(idx, E_ROUTED, dtype=x.dtype) * scores[..., None]).sum(-2)
        out = shared
        for e in range(E_ROUTED):
            out = out + cw[..., e:e + 1] * _expert(x, Wg[e], Wu[e], Wd[e])
        return out
    x = L0_attn_x
    x = _layernorm(x + _L0_attn_ref(x, L0_attn_Wattn, L0_attn_battn, L0_attn_Wproj, L0_attn_bproj, L0_attn_embk, L0_attn_embv), axis=-1)
    x = _layernorm(x + _L0_ffn_ref(x, L0_ffn_Wg_s, L0_ffn_Wu_s, L0_ffn_Wd_s, L0_ffn_Wg, L0_ffn_Wu, L0_ffn_Wd, L0_ffn_Wr, L0_ffn_rb), axis=-1)
    return x

_drawn_inputs = setup_inputs


def setup_inputs(seed=0):
    import zlib

    import numpy as np

    out = dict(_drawn_inputs(seed))
    spreads = {'L0_ffn_rb': (0.0, 0.8)}
    factors = {'L0_attn_Wattn': 7.242,
     'L0_attn_battn': 8.0,
     'L0_attn_Wproj': 6.179,
     'L0_attn_bproj': 2.747,
     'L0_attn_embk': 8.0,
     'L0_attn_embv': 8.0,
     'L0_ffn_Wg_s': 6.703,
     'L0_ffn_Wu_s': 6.509,
     'L0_ffn_Wd_s': 6.449,
     'L0_ffn_Wg': 8.0,
     'L0_ffn_Wu': 8.0,
     'L0_ffn_Wd': 8.0,
     'L0_ffn_Wr': 8.0}
    for name, (base, spread) in spreads.items():
        noise = np.random.default_rng([zlib.crc32(name.encode()), seed]).standard_normal(out[name].shape)
        drawn = base * np.exp(spread * noise) if base else spread * noise
        out[name] = jnp.asarray(drawn.astype(out[name].dtype))
    for name, factor in factors.items():
        out[name] = (out[name] * factor).astype(out[name].dtype)
    return out
```

```python
from contextlib import ExitStack

import concourse.bass as bass
from concourse import mybir

ALU = mybir.AluOpType
ACT = mybir.ActivationFunctionType
AX = mybir.AxisListType
F32 = mybir.dt.float32
F16 = mybir.dt.float16
BF16 = mybir.dt.bfloat16

P = 128
EPS = 1e-5


def attention_and_experts(nc, x, xT, Wqkv, bq, bk, bv, Wp, bp, ekrev, evrev, Wup, Wdn, WrT, rb,
                          ident_in, m8_in, mh_in, sel8_in, causal_in, tri_in, out):
    B, T, C = x.shape
    H = 16
    D = C // H
    REL = T - P
    G = T // 8
    PAIRS = G // 2
    SCALE = 1.0 / float(D) ** 0.5
    E1 = Wup.shape[2]
    E = E1 - 1
    I = Wup.shape[3]
    TILES = B * T // P
    assert C == P and T == 2 * P and D == 8 and I == 2 * P and REL == P

    outer = ExitStack()
    with outer:
        def sem(name):
            return outer.enter_context(nc.semaphore(name))

        def keep(name, shape, dt):
            return outer.enter_context(nc.sbuf_tensor(name, shape, dt))

        R = keep("R", [P, TILES, C], F32)
        wup32 = keep("wup32", [P, 2, E1, I], F32)
        wdn32 = keep("wdn32", [P, E1, 2, C], F32)
        wr32 = keep("wr32", [P, E], F32)
        rb_bc = keep("rb_bc", [P, E], F32)
        ident = keep("ident", [P, P], F32)
        eps_col = keep("eps_col", [P, 1], F32)
        tri = keep("tri", [P, E, E], F32)

        moe_weights_in = sem("moe_weights_in")
        const_in = sem("const_in")

        att = ExitStack()
        with att:
            def sb(name, shape, dt):
                return att.enter_context(nc.sbuf_tensor(name, shape, dt))

            wqkv = sb("wqkv", [P, 3 * C], F32)
            wp = sb("wp", [P, C], F32)
            bq_col = sb("bq_col", [P, 1], F32)
            bk_col = sb("bk_col", [P, 1], F32)
            bks_col = sb("bks_col", [P, 1], F32)
            bv_bc = sb("bv_bc", [P, C], F32)
            bp_bc = sb("bp_bc", [P, C], F32)
            m8 = sb("m8", [P, P], F16)
            mh = sb("mh", [P, P], F16)
            sel8 = sb("sel8", [P, P], BF16)
            causal = sb("causal", [P, 24], BF16)
            ESW = T + 8
            ek32 = sb("ek32", [P, ESW], F32)
            ekh = sb("ekh", [P, ESW], F16)
            ekl = sb("ekl", [P, ESW], F16)
            ev = sb("ev", [P, T, D], F32)
            evw = sb("evw", [P, 2, 16, 8, D], F32)
            xTb = [sb(f"xTb{i}", [P, T], F32) for i in range(2)]
            xb = sb("xb", [P, 2, C], F32)
            qs = sb("qs", [P, 2, T], F16)
            qbd = [sb(f"qbd{i}", [P, 2, G, P], F16) for i in range(2)]
            q2rep = sb("q2rep", [P, H, T], F16)
            q2 = [sb(f"q2_{i}", [P, G, P], F16) for i in range(2)]
            kf = sb("kf", [P, T], F32)
            khi = [sb(f"khi{i}", [P, T], F16) for i in range(2)]
            klo = [sb(f"klo{i}", [P, T], F16) for i in range(2)]
            v1 = [sb(f"v1_{i}", [P, 2, H, 32], F32) for i in range(2)]
            nmax = sb("nmax", [P, G], F32)
            WB = [P * (g // (G // 2) + 1) for g in range(G)]
            PB = [sum(WB[:g]) for g in range(G)]
            prob = sb("prob", [P, sum(WB)], F32)
            pt0 = sb("pt0", [P, G * P], F32)
            pt1 = sb("pt1", [P, G * P // 2], F32)
            z1 = sb("z1", [P, H // 4, T], F32)
            z2 = sb("z2", [P, H, 8, 16], F32)
            yT1 = sb("yT1", [P, T], F32)
            yT2 = sb("yT2", [P, T], F32)
            den = sb("den", [P, T], F32)
            ysum = sb("ysum", [P, T], F32)
            rden = sb("rden", [P, T], F32)
            yT = sb("yT", [P, T], F32)
            xpb = sb("xpb", [P, 2, C], F32)

            S = [att.enter_context(nc.psum_tensor(f"S{i}", [P, 512], F32)) for i in range(4)]
            TB = [att.enter_context(nc.psum_tensor(f"TB{i}", [P, 512], F32)) for i in range(3)]
            XB = att.enter_context(nc.psum_tensor("XB", [P, 512], F32))

            qd = [nc.dram_tensor(f"qd{i}", [2, H, D, T], F16, kind="Internal").ap() for i in range(2)]
            y1d = [nc.dram_tensor(f"y1d{i}", [H, D, T], F32, kind="Internal").ap() for i in range(2)]
            dnd = [nc.dram_tensor(f"dnd{i}", [H, D, T], F32, kind="Internal").ap() for i in range(2)]
            y2d = [nc.dram_tensor(f"y2d{i}", [H, D, T], F32, kind="Internal").ap() for i in range(2)]

            early_in = sem("early_in")
            zeroed = sem("zeroed")
            ek_ready = sem("ek_ready")
            bks_ready = sem("bks_ready")
            xT_in = [sem("xT_in0"), sem("xT_in1")]
            xb_in = sem("xb_in")
            qk_ready = sem("qk_ready")
            hi_done = sem("hi_done")
            qlo_done = sem("qlo_done")
            kf_done = sem("kf_done")
            klo_done = sem("klo_done")
            v_ready = sem("v_ready")
            v_done = sem("v_done")
            qbd_done = sem("qbd_done")
            evw_ready = sem("evw_ready")
            q_spill = sem("q_spill")
            q2rep_in = sem("q2rep_in")
            q2_done = sem("q2_done")
            score_ready = sem("score_ready")
            max_done = sem("max_done")
            exp_done = sem("exp_done")
            tr_ready = sem("tr_ready")
            tr_out_a = sem("tr_out_a")
            tr_out_v = sem("tr_out_v")
            y_ready = sem("y_ready")
            y_out_a = sem("y_out_a")
            y_out_v = sem("y_out_v")
            y_spill = sem("y_spill")
            y_back = sem("y_back")
            ysum_done = sem("ysum_done")
            rden_done = sem("rden_done")
            yT_done = sem("yT_done")
            xpb_done = sem("xpb_done")
            proj_ready = sem("proj_ready")
            r_done = sem("r_done")

            GROUPS = []
            for q in range(4):
                for blk in range(1 + q // 2):
                    GROUPS += [(8 * q, blk), (8 * q + 4, blk)]
            NG = len(GROUPS)
            OF_STRIP = [[k for k, (g, _) in enumerate(GROUPS) if g // 8 == q] for q in range(4)]
            Y_SPILLS = 8 + 16

            def pair_out_waits(eng, n):
                if not (isinstance(n, int) and n == 0):
                    eng.wait_ge(y_out_a, n * 3)
                    eng.wait_ge(y_out_v, n * 3)

            def group_out_wait(eng, n, k):
                if k >= 3:
                    if (k - 3) % 2 == 0:
                        eng.wait_ge(tr_out_a, n * 6 + (k - 3) // 2 + 1)
                    else:
                        eng.wait_ge(tr_out_v, n * 6 + (k - 3) // 2 + 1)
                elif not (isinstance(n, int) and n == 0):
                    kk = NG + k - 3
                    if kk % 2 == 0:
                        eng.wait_ge(tr_out_a, n * 6 - 6 + kk // 2 + 1)
                    else:
                        eng.wait_ge(tr_out_v, n * 6 - 6 + kk // 2 + 1)

            block = att.enter_context(nc.Block())

            @block.sync
            def _(sp):
                def load_xT(m, par):
                    sp.dma_start(xTb[par][:, :], xT[:, bass.ds(m * T, T)]).then_inc(xT_in[par], 16)

                def load_xb(n):
                    sp.dma_start(xb[:, :, :], x[bass.ds(n, 1), :, :].rearrange(
                        "o (i p) c -> p (o i) c", p=P)).then_inc(xb_in, 16)

                def spill_q(m, par):
                    sp.wait_ge(qlo_done, m + 1)
                    sp.dma_start(qd[par].rearrange("a h d t -> (h d) a t"), qs[:, :, :]).then_inc(q_spill, 16)

                def spread_q(m, par):
                    sp.wait_ge(q_spill, m * 16 + 16)
                    if not (isinstance(m, int) and m == 0):
                        sp.wait_ge(q2_done, m)
                    for a in range(2):
                        for t in range(8):
                            r = 64 * a + D * t
                            sp.dma_start(q2rep[r:r + D, :, :],
                                         qd[par][a].rearrange("h d t -> d h t")).then_inc(q2rep_in, 16)

                def spill_y(n, par):
                    sp.wait_ge(y_out_a, n * 3 + 3)
                    sp.wait_ge(y_out_v, n * 3 + 3)
                    for hq in range(4):
                        for dst, r in ((y1d, 0), (dnd, D)):
                            sp.dma_start(dst[par].rearrange("(j q) d t -> q d j t", q=4)[hq],
                                         z1[32 * hq + r:32 * hq + r + D, :, :]).then_inc(y_spill, 16)
                    for half in range(2):
                        for r in range(8):
                            row, tt = 64 * half + D * r, 7 - r
                            at = P * half + 16 * tt
                            sp.dma_start(y2d[par].rearrange("h d t -> d h t")[:, :, at:at + 16],
                                         z2[row:row + D, :, tt, :]).then_inc(y_spill, 16)

                def back_y(n, par):
                    sp.wait_ge(y_spill, (n + 1) * (16 * Y_SPILLS))
                    sp.wait_ge(yT_done, n + 1)
                    for dst, src in ((yT1, y1d), (den, dnd), (yT2, y2d)):
                        sp.dma_start(dst[:, :], src[par].rearrange("h d t -> (h d) t")).then_inc(y_back, 16)

                def step(n, par, first=False, last=False):
                    if not last:
                        if not first:
                            sp.wait_ge(v_ready, n)
                        load_xT(n + 1, 1 - par)
                    if not first:
                        sp.wait_ge(xpb_done, n)
                    load_xb(n)
                    if not first:
                        spill_y(n - 1, 1 - par)
                    if not last:
                        spill_q(n + 1, 1 - par)
                    if not first:
                        back_y(n - 1, 1 - par)
                    if not last:
                        spread_q(n + 1, 1 - par)

                load_xT(0, 0)
                sp.dma_start(wqkv[:, :], Wqkv).then_inc(early_in, 16)
                sp.dma_start(bq_col[:, :], bq).then_inc(early_in, 16)
                sp.dma_start(bk_col[:, :], bk).then_inc(early_in, 16)
                sp.dma_start(bv_bc[:, :], bv.partition_broadcast(P)).then_inc(early_in, 16)
                spill_q(0, 0)
                spread_q(0, 0)
                step(0, 0, first=True)
                with sp.Fori(0, B // 2 - 1, 1) as i:
                    step(i * 2 + 1, 1)
                    step(i * 2 + 2, 0)
                step(B - 1, 1, last=True)
                spill_y(B - 1, 1)
                back_y(B - 1, 1)

            @block.gpsimd
            def _(pool):
                for dst, src in ((m8, m8_in), (mh, mh_in), (sel8, sel8_in), (causal, causal_in), (ident, ident_in),
                                 (wp, Wp)):
                    pool.dma_start(dst[:, :], src).then_inc(const_in, 16)
                for a in range(2):
                    for t in range(8):
                        r = 64 * a + D * t
                        pool.dma_start(ek32[r:r + D, :], ekrev[:, 7 - t:7 - t + ESW]).then_inc(const_in, 16)
                pool.dma_start(ev[:, :, :].rearrange("p y d -> p (y d)"),
                               bass.AP(evrev.tensor, evrev.offset, [[D, P], [1, T * D]])).then_inc(const_in, 16)
                pool.dma_start(bp_bc[:, :], bp.partition_broadcast(P)).then_inc(const_in, 16)
                pool.dma_start(wup32[:, :, :, :], Wup).then_inc(moe_weights_in, 16)
                pool.dma_start(wdn32[:, :, :, :], Wdn).then_inc(moe_weights_in, 16)
                pool.dma_start(wr32[:, :], WrT).then_inc(moe_weights_in, 16)
                pool.dma_start(rb_bc[:, :], rb.partition_broadcast(P)).then_inc(moe_weights_in, 16)
                pool.dma_start(tri[:, :, :].rearrange("p a b -> p (a b)"), tri_in).then_inc(moe_weights_in, 16)
                nc.gpsimd.memset(prob[:, :], 0.0).then_inc(zeroed, 1)
                pool.wait_ge(const_in, CONSTS)

                def step(n):
                    pool.wait_ge(xb_in, n * 16 + 16)
                    pool.wait_ge(r_done, n + 1)
                    nc.gpsimd.tensor_tensor(xpb[:, :, :], xb[:, :, :], bp_bc[:, :].unsqueeze(1).broadcast_to([P, 2, C]),
                                            ALU.add).then_inc(xpb_done, 1)

                with pool.Fori(0, B, 1) as n:
                    step(n)

            @block.tensor
            def _(pe):
                def project_qk(m, par, halfm):
                    pe.wait_ge(xT_in[par], halfm * 16 + 16)
                    if not (isinstance(m, int) and m < 2):
                        pe.wait_ge(r_done, m - 1)
                    nc.tensor.matmul(XB[:, 0:T], wqkv[:, 0:C], xTb[par][:, :], start=True, stop=True)
                    nc.tensor.matmul(XB[:, T:2 * T], wqkv[:, C:2 * C], xTb[par][:, :], start=True,
                                     stop=True).then_inc(qk_ready, 1)

                def project_v(m, par):
                    pe.wait_ge(kf_done, m + 1)
                    nc.tensor.matmul(XB[:, 0:C], xTb[par][:, 0:P], wqkv[:, 2 * C:3 * C], start=True, stop=True)
                    nc.tensor.matmul(XB[:, C:2 * C], xTb[par][:, P:T], wqkv[:, 2 * C:3 * C], start=True,
                                     stop=True).then_inc(v_ready, 1)

                def project_out(n, m):
                    pe.wait_ge(yT_done, n + 2)
                    pe.wait_ge(v_done, m)
                    nc.tensor.matmul(XB[:, 0:C], yT[:, 0:P], wp[:, :], start=True, stop=True)
                    nc.tensor.matmul(XB[:, C:2 * C], yT[:, P:T], wp[:, :], start=True,
                                     stop=True).then_inc(proj_ready, 1)

                def scores(n, par, pairs):
                    for j in pairs:
                        bank = S[j % 4]
                        if j >= 4:
                            pe.wait_ge(exp_done, n * PAIRS + j - 3)
                        W2 = 16 * (j + 1)
                        for a in range(2):
                            g = 2 * j + a
                            o = bank[:, 256 * a:256 * a + W2]
                            qh = qbd[par][:, 0, g, :]
                            ql = qbd[par][:, 1, g, :]
                            qr = q2[par][:, g, :]
                            off = T - 8 - 8 * g
                            nc.tensor.matmul(o, qh, khi[par][:, 0:W2], start=(a == 0), stop=False, skip_group_check=True)
                            nc.tensor.matmul(o, qh, klo[par][:, 0:W2], start=False, stop=False, skip_group_check=True)
                            nc.tensor.matmul(o, ql, khi[par][:, 0:W2], start=False, stop=False, skip_group_check=True)
                            nc.tensor.matmul(o, qr, ekh[:, off:off + W2], start=False, stop=False, skip_group_check=True)
                            nc.tensor.matmul(o, qr, ekl[:, off:off + W2], start=False, stop=False, skip_group_check=True)
                            last = nc.tensor.matmul(o[:, W2 - 16:W2], sel8[:, :], causal[:, 8 - 8 * a:24 - 8 * a],
                                                    start=False, stop=True, skip_group_check=True)
                        last.then_inc(score_ready, 1)

                def turn(n, groups):
                    for k in groups:
                        g0, blk = GROUPS[k]
                        pe.wait_ge(exp_done, n * PAIRS + g0 // 2 + 2)
                        group_out_wait(pe, n, k)
                        for i in range(4):
                            at = PB[g0 + i] + P * blk
                            last = nc.tensor.transpose(TB[k % 3][:, P * i:P * i + P], prob[:, at:at + P],
                                                       ident[:, :])
                        last.then_inc(tr_ready, 1)

                def bank_free(n, k):
                    if k >= 4:
                        if k % 2 == 0:
                            pe.wait_ge(y_out_a, n * 3 + (k - 4) // 2 + 1)
                        else:
                            pe.wait_ge(y_out_v, n * 3 + (k - 4) // 2 + 1)

                def outputs(n, par):
                    p0 = pt0[:, :].rearrange("p (g h t) -> p g h t", h=H, t=8)
                    p1 = pt1[:, :].rearrange("p (g h t) -> p g h t", h=H, t=8)
                    pe.wait_ge(tr_out_a, n * 6 + 6)
                    pe.wait_ge(tr_out_v, n * 6 + 6)
                    for k in range(2):
                        for jj in range(2):
                            for blk in range(2):
                                for hq in range(4):
                                    h = 4 * (2 * k + jj) + hq
                                    if blk == 0:
                                        o, r = S[k][32 * hq:32 * hq + 32, T * jj:T * jj + T], p0[:, :, h, :]
                                    else:
                                        o, r = S[k][32 * hq:32 * hq + 32, T * jj + P:T * jj + T], p1[:, :, h, :]
                                    last = nc.tensor.matmul(o, v1[par][:, blk, h, :], r, start=(jj == 0 and blk == 0),
                                                            stop=(blk == 1), skip_group_check=True,
                                                            tile_position=(0, 32 * hq))
                        last.then_inc(y_ready, 1)
                    p0 = pt0[:, :].rearrange("p (b tt a h t) -> p b tt a h t", b=2, a=2, h=H, t=8)
                    p1 = pt1[:, :].rearrange("p (tt a h t) -> p tt a h t", a=2, h=H, t=8)
                    for k in range(2, 6):
                        bank_free(n, k)
                        for jj in range(4):
                            j = 4 * (k - 2) + jj
                            for half, blk in ((0, 0), (1, 0), (1, 1)):
                                lhs = evw[:, 1 - (half - blk), 15 - j, :, :].rearrange("p r d -> p (r d)")
                                src = p1[:, :, j // 8, :, j % 8] if blk else p0[:, half, :, j // 8, :, j % 8]
                                last = nc.tensor.matmul(S[k % 4][64 * half:64 * half + 64, P * jj:P * jj + P], lhs, src,
                                                        start=(jj == 0 and blk == 0), stop=(half == blk),
                                                        skip_group_check=True, tile_position=(0, 64 * half))
                        last.then_inc(y_ready, 1)

                def step(n, par, halfm, first=False, last=False):
                    pe.wait_ge(qbd_done, n * 2 + 2)
                    pe.wait_ge(klo_done, n + 1)
                    pe.wait_ge(q2_done, n + 1)
                    pe.wait_ge(v_done, n + 1)
                    if not last:
                        project_qk(n + 1, 1 - par, halfm)
                    pair_out_waits(pe, n)
                    scores(n, par, range(0, 4))
                    if not last:
                        project_v(n + 1, 1 - par)
                    scores(n, par, range(4, 8))
                    turn(n, OF_STRIP[0])
                    scores(n, par, range(8, 12))
                    turn(n, OF_STRIP[1])
                    scores(n, par, range(12, 14))
                    if not first:
                        project_out(n - 1, n + 1 if last else n + 2)
                    turn(n, OF_STRIP[2])
                    scores(n, par, range(14, 16))
                    turn(n, OF_STRIP[3])
                    outputs(n, par)

                pe.wait_ge(early_in, 64)
                project_qk(0, 0, 0)
                project_v(0, 0)
                pe.wait_ge(const_in, CONSTS)
                pe.wait_ge(ek_ready, 2)
                pe.wait_ge(evw_ready, 2)
                pe.wait_ge(zeroed, ZEROS)
                step(0, 0, 0, first=True)
                with pe.Fori(0, B // 2 - 1, 1) as i:
                    step(i * 2 + 1, 1, i + 1)
                    step(i * 2 + 2, 0, i + 1)
                step(B - 1, 1, 0, last=True)
                project_out(B - 1, B)

            @block.scalar
            def _(act):
                def split_hi(m, par):
                    act.wait_ge(qk_ready, m + 1)
                    if not (isinstance(m, int) and m == 0):
                        act.wait_ge(qbd_done, m * 2)
                        act.wait_ge(q_spill, m * 16)
                    nc.scalar.activation(qs[:, 0, :], XB[:, 0:T], ACT.Identity, bias=bq_col[:, 0:1])
                    nc.scalar.activation(khi[par][:, :], XB[:, T:2 * T], ACT.Identity, bias=bks_col[:, 0:1],
                                         scale=SCALE).then_inc(hi_done, 1)

                def exps(n, pairs):
                    for j in pairs:
                        act.wait_ge(max_done, n * PAIRS + j + 1)
                        W2 = 16 * (j + 1)
                        for a in range(2):
                            g = 2 * j + a
                            last = nc.scalar.activation(prob[:, PB[g]:PB[g] + W2], S[j % 4][:, 256 * a:256 * a + W2],
                                                        ACT.Exp, bias=nmax[:, g:g + 1])
                        last.then_inc(exp_done, 1)

                def turned(n, groups):
                    for k in groups:
                        if k % 2 == 0:
                            g0, blk = GROUPS[k]
                            act.wait_ge(tr_ready, n * NG + k + 1)
                            dst = pt1[:, P * (g0 - G // 2):P * (g0 - G // 2) + 512] if blk else \
                                pt0[:, P * g0:P * g0 + 512]
                            nc.scalar.activation(dst, TB[k % 3][:, :], ACT.Copy).then_inc(tr_out_a, 1)

                def step(n, par, first=False, last=False):
                    if not last:
                        split_hi(n + 1, 1 - par)
                    exps(n, range(0, 8))
                    turned(n, OF_STRIP[0])
                    exps(n, range(8, 12))
                    turned(n, OF_STRIP[1])
                    exps(n, range(12, 14))
                    turned(n, OF_STRIP[2])
                    exps(n, range(14, 16))
                    turned(n, OF_STRIP[3])
                    if not first:
                        act.wait_ge(y_spill, n * (16 * Y_SPILLS))
                    act.wait_ge(y_ready, n * 6 + 1)
                    nc.scalar.activation(z1[:, 0:2, :], S[0][:, :], ACT.Copy).then_inc(y_out_a, 1)
                    for k in (2, 4):
                        act.wait_ge(y_ready, n * 6 + k + 1)
                        j0 = 4 * (k - 2)
                        nc.scalar.activation(z2[:, :, :, j0:j0 + 4].rearrange("p h t j -> p j t h"),
                                             S[k % 4][:, :].rearrange("p (j t h) -> p j t h", j=4, t=8),
                                             ACT.Copy).then_inc(y_out_a, 1)

                act.wait_ge(early_in, 64)
                act.wait_ge(bks_ready, 1)
                split_hi(0, 0)
                act.wait_ge(zeroed, ZEROS)
                step(0, 0, first=True)
                with act.Fori(0, B // 2 - 1, 1) as i:
                    step(i * 2 + 1, 1)
                    step(i * 2 + 2, 0)
                step(B - 1, 1, last=True)

            @block.vector
            def _(dve):
                def split_lo(m, par):
                    dve.wait_ge(hi_done, m + 1)
                    nc.vector.scalar_tensor_tensor(out=qs[:, 1, :], in0=XB[:, 0:T], scalar=bq_col[:, 0:1],
                                                   in1=qs[:, 0, :], op0=ALU.add, op1=ALU.subtract).then_inc(qlo_done, 1)
                    if not (isinstance(m, int) and m == 0):
                        dve.wait_ge(klo_done, m)
                    nc.vector.tensor_scalar(kf[:, :], XB[:, T:2 * T], bk_col[:, 0:1], SCALE, ALU.add,
                                            ALU.mult).then_inc(kf_done, 1)
                    dve.wait_ge(kf_done, m + 1)
                    nc.vector.tensor_tensor(klo[par][:, :], kf[:, :], khi[par][:, :],
                                            ALU.subtract).then_inc(klo_done, 1)

                def take_v(m, par):
                    dve.wait_ge(v_ready, m + 1)
                    nc.vector.tensor_tensor(v1[par][:, :, :, 0:D],
                                            XB[:, 0:2 * C].rearrange("p (b h d) -> p b h d", b=2, h=H),
                                            bv_bc[:, :].rearrange("p (h d) -> p h d", h=H).unsqueeze(1)
                                            .broadcast_to([P, 2, H, D]), ALU.add).then_inc(v_done, 1)

                def mask_q2(m, par):
                    dve.wait_ge(q2rep_in, (m + 1) * (16 * 16))
                    nc.vector.tensor_tensor(q2[par][:, :, :].rearrange("p g (h t) -> p g h t", h=H),
                                            q2rep[:, :, :].rearrange("p h (g t) -> p g h t", t=8),
                                            m8[:, :].rearrange("p (h t) -> p h t", h=H).unsqueeze(1)
                                            .broadcast_to([P, G, H, 8]), ALU.mult).then_inc(q2_done, 1)

                def mask_q(m, par):
                    dve.wait_ge(qlo_done, m + 1)
                    for a in range(2):
                        nc.vector.tensor_tensor(qbd[par][:, a, :, :].rearrange("p g (h t) -> p g h t", h=H),
                                                qs[:, a, :].rearrange("p (g t) -> p g t", t=8).unsqueeze(2)
                                                .broadcast_to([P, G, H, 8]),
                                                mh[:, :].rearrange("p (h t) -> p h t", h=H).unsqueeze(1)
                                                .broadcast_to([P, G, H, 8]), ALU.mult).then_inc(qbd_done, 1)

                def maxima(n, pairs):
                    for j in pairs:
                        W2 = 16 * (j + 1)
                        dve.wait_ge(score_ready, n * PAIRS + j + 1)
                        nc.vector.tensor_reduce(nmax[:, 2 * j:2 * j + 2],
                                                S[j % 4][:, :].rearrange("p (a w) -> p a w", a=2)[:, :, 0:W2],
                                                AX.X, ALU.max, negate=True).then_inc(max_done, 1)

                def turned(n, groups):
                    for k in groups:
                        if k % 2:
                            g0, blk = GROUPS[k]
                            dve.wait_ge(tr_ready, n * NG + k + 1)
                            dst = pt1[:, P * (g0 - G // 2):P * (g0 - G // 2) + 512] if blk else \
                                pt0[:, P * g0:P * g0 + 512]
                            nc.vector.tensor_copy(dst, TB[k % 3][:, :]).then_inc(tr_out_v, 1)

                def normalise(n):
                    dve.wait_ge(y_back, n * 48 + 48)
                    nc.vector.tensor_tensor(ysum[:, :], yT1[:, :], yT2[:, :], ALU.add).then_inc(ysum_done, 1)
                    nc.vector.reciprocal(rden[:, :], den[:, :]).then_inc(rden_done, 1)
                    dve.wait_ge(ysum_done, n + 1)
                    dve.wait_ge(rden_done, n + 1)
                    nc.vector.tensor_tensor(yT[:, :], ysum[:, :], rden[:, :], ALU.mult).then_inc(yT_done, 1)

                def residual(n):
                    dve.wait_ge(proj_ready, n + 1)
                    dve.wait_ge(xpb_done, n + 1)
                    nc.vector.tensor_tensor(R[:, bass.ds(n * 2, 2), :], XB[:, 0:2 * C].rearrange("p (i c) -> p i c", i=2),
                                            xpb[:, :, :], ALU.add).then_inc(r_done, 1)

                def step(n, par, first=False, last=False):
                    if not last:
                        split_lo(n + 1, 1 - par)
                    maxima(n, range(0, 4))
                    if not last:
                        take_v(n + 1, 1 - par)
                    maxima(n, range(4, 8))
                    turned(n, OF_STRIP[0])
                    if not last:
                        mask_q(n + 1, 1 - par)
                    maxima(n, range(8, 12))
                    if not first:
                        normalise(n - 1)
                    turned(n, OF_STRIP[1])
                    maxima(n, range(12, 14))
                    if not first:
                        residual(n - 1)
                    turned(n, OF_STRIP[2])
                    maxima(n, range(14, 16))
                    if not last:
                        mask_q2(n + 1, 1 - par)
                    turned(n, OF_STRIP[3])
                    if not first:
                        dve.wait_ge(y_spill, n * (16 * Y_SPILLS))
                    dve.wait_ge(y_ready, n * 6 + 2)
                    nc.vector.tensor_copy(z1[:, 2:4, :], S[1][:, :].rearrange("p (j t) -> p j t", j=2)).then_inc(y_out_v, 1)
                    for k in (3, 5):
                        dve.wait_ge(y_ready, n * 6 + k + 1)
                        j0 = 4 * (k - 2)
                        nc.vector.tensor_copy(z2[:, :, :, j0:j0 + 4].rearrange("p h t j -> p j t h"),
                                              S[k % 4][:, :].rearrange("p (j t h) -> p j t h", j=4, t=8)).then_inc(y_out_v, 1)

                for par in range(2):
                    nc.vector.memset(v1[par][:, :, :, D:32], 1.0).then_inc(zeroed, 1)
                nc.vector.memset(eps_col[:, :], EPS).then_inc(r_done, 1)
                nc.vector.memset(yT[:, :], 0.0).then_inc(yT_done, 1)
                nc.vector.memset(ekl[64:P, :], 0.0).then_inc(zeroed, 1)
                dve.wait_ge(early_in, 64)
                nc.vector.tensor_scalar(bks_col[:, :], bk_col[:, :], SCALE, None, ALU.mult).then_inc(bks_ready, 1)
                split_lo(0, 0)
                take_v(0, 0)
                dve.wait_ge(const_in, CONSTS)
                nc.vector.tensor_copy(ekh[:, :], ek32[:, :]).then_inc(ek_ready, 1)
                dve.wait_ge(ek_ready, 1)
                nc.vector.tensor_tensor(ekl[0:64, :], ek32[0:64, :], ekh[0:64, :], ALU.subtract).then_inc(ek_ready, 1)
                for b in range(2):
                    nc.vector.tensor_copy(evw[:, b, :, :, :], ev[:, P * b:P * b + P, :].rearrange(
                        "p (r j) d -> p j r d", j=16)).then_inc(evw_ready, 1)
                mask_q(0, 0)
                mask_q2(0, 0)
                step(0, 0, first=True)
                with dve.Fori(0, B // 2 - 1, 1) as i:
                    step(i * 2 + 1, 1)
                    step(i * 2 + 2, 0)
                step(B - 1, 1, last=True)
                normalise(B - 1)
                residual(B - 1)

        experts(nc, sem, E, E1, I, TILES, R, wup32, wdn32, wr32, rb_bc, ident, eps_col, tri,
                moe_weights_in, out)


CONSTS = 16 * (6 + 16 + 2)
ZEROS = 1 + 3


def experts(nc, sem, E, E1, I, TILES, R, wup32, wdn32, wr32, rb_bc, ident, eps_col, tri,
            moe_weights_in, out):
    C = P
    CH = 4
    NCH = TILES // CH
    TOK = CH * P
    ctx = ExitStack()
    with ctx:
        def sb(name, shape, dt):
            return ctx.enter_context(nc.sbuf_tensor(name, shape, dt))

        def ps(name):
            return ctx.enter_context(nc.psum_tensor(name, [P, 512], F32))

        stats = sb("lnstats", [P, TILES, 6], F32)
        mv = sb("mv", [P, TILES, 2], F32)
        mv2 = sb("mv2", [P, TILES, 2], F32)
        std = sb("std", [P, TILES], F32)
        rstd = sb("rstd", [P, TILES], F32)
        std2 = sb("std2", [P, TILES], F32)
        rstd2 = sb("rstd2", [P, TILES], F32)
        wuph = sb("wuph", [P, 2, E1, I], F16)
        wupl = sb("wupl", [P, 2, E1, I], F16)
        wrh = sb("wrh", [P, E], F16)
        wrl = sb("wrl", [P, E], F16)
        xT32 = sb("xT32", [P, TILES * P], F32)
        xTh = sb("xTh", [P, TILES * P], F16)
        xTl = sb("xTl", [P, TILES * P], F16)
        logit = sb("logit", [P, TILES, E], F32)
        pr = sb("pr", [P, TILES, E], F32)
        gt = sb("gt", [P, TILES, E, E], F32)
        eq = sb("eq", [P, TILES, E, E], F32)
        rank = sb("rank", [P, TILES, E], F32)
        cw = sb("cw", [P, TILES, E1], F32)
        sg = [sb(f"sg{i}", [P, TOK], F32) for i in range(3)]
        hid = [sb(f"hid{i}", [P, TOK], F32) for i in range(6)]

        GB = [ps(f"GB{i}") for i in range(3)]
        UB = [ps(f"UB{i}") for i in range(3)]
        DB = [ps(f"DB{i}") for i in range(2)]

        w_split = sem("w_split")
        st1 = sem("st1")
        mv_done = sem("mv_done")
        std_done = sem("std_done")
        rstd_done = sem("rstd_done")
        ln_done = sem("ln_done")
        xt_ready = sem("xt_ready")
        xt_out = sem("xt_out")
        xh_done = sem("xh_done")
        xl_done = sem("xl_done")
        logit_ready = sem("logit_ready")
        logit_done = sem("logit_done")
        pr_done = sem("pr_done")
        rank_steps = sem("rank_steps")
        cw_done = sem("cw_done")
        up_ready = sem("up_ready")
        silu_done = sem("silu_done")
        hid_done = sem("hid_done")
        down_ready = sem("down_ready")
        acc_done = sem("acc_done")
        st2 = sem("st2")
        mv2_done = sem("mv2_done")
        std2_done = sem("std2_done")
        rstd2_done = sem("rstd2_done")
        fin_done = sem("fin_done")
        stored = sem("stored")

        UNITS = 2 * E1
        block = ctx.enter_context(nc.Block())

        @block.sync
        def _(sp):
            o = out.rearrange("b (i p) c -> p (b i) c", p=P)
            for c in range(NCH):
                sp.wait_ge(fin_done, CH * (c + 1))
                sp.dma_start(o[:, CH * c:CH * c + CH, :], R[:, CH * c:CH * c + CH, :]).then_inc(stored, 16)
            sp.wait_ge(stored, 16 * NCH)

        @block.tensor
        def _(pe):
            for c in range(NCH):
                pe.wait_ge(ln_done, CH * (c + 1))
                if c >= 2:
                    pe.wait_ge(xt_out, c - 1)
                for i in range(CH):
                    last = nc.tensor.transpose(DB[c % 2][:, P * i:P * i + P], R[:, CH * c + i, :], ident[:, :])
                last.then_inc(xt_ready, 1)
            pe.wait_ge(w_split, 6)
            pe.wait_ge(xl_done, NCH)
            for t in range(TILES):
                o = GB[2][:, E * t:E * t + E]
                xh, xl = xTh[:, P * t:P * t + P], xTl[:, P * t:P * t + P]
                nc.tensor.matmul(o, xh, wrh[:, :], start=(t == 0), stop=False, skip_group_check=True)
                nc.tensor.matmul(o, xh, wrl[:, :], start=False, stop=False, skip_group_check=True)
                last = nc.tensor.matmul(o, xl, wrh[:, :], start=False, stop=True, skip_group_check=True)
            last.then_inc(logit_ready, 1)
            pe.wait_ge(xt_out, NCH)

            def up(c, e, k):
                u = 2 * e + k
                if u >= 3 or not isinstance(c, int) or c > 0:
                    pe.wait_ge(hid_done, c * UNITS + u - 2)
                if u == 2:
                    pe.wait_ge(logit_done, 1)
                for w, bank in ((0, GB[u % 3]), (1, UB[u % 3])):
                    wh = wuph[:, w, e, P * k:P * k + P]
                    wl = wupl[:, w, e, P * k:P * k + P]
                    nc.tensor.matmul(bank[:, :], wh, xTh[:, bass.ds(c * TOK, TOK)], start=True, stop=False)
                    nc.tensor.matmul(bank[:, :], wh, xTl[:, bass.ds(c * TOK, TOK)], start=False, stop=False)
                    last = nc.tensor.matmul(bank[:, :], wl, xTh[:, bass.ds(c * TOK, TOK)], start=False, stop=True)
                last.then_inc(up_ready, 1)

            def down(c, e, par):
                pe.wait_ge(hid_done, c * UNITS + 2 * e + 2)
                if not (isinstance(c, int) and c == 0 and e < 2):
                    pe.wait_ge(acc_done, (c * E1 + e - 1) * CH)
                for i in range(CH):
                    for k in range(2):
                        u = 2 * e + k
                        last = nc.tensor.matmul(DB[(e + par) % 2][:, P * i:P * i + P], hid[u % 6][:, P * i:P * i + P],
                                                wdn32[:, e, k, :], start=(k == 0), stop=(k == 1))
                last.then_inc(down_ready, 1)

            def chunk(c, par):
                for e in range(E1):
                    up(c, e, 0)
                    up(c, e, 1)
                    if e:
                        down(c, e - 1, par)
                down(c, E1 - 1, par)

            chunk(0, 0)
            chunk(1, 1)
            with pe.Fori(1, NCH // 2, 1) as i:
                chunk(i * 2, 0)
                chunk(i * 2 + 1, 1)

        @block.scalar
        def _(act):
            act.wait_ge(mv_done, TILES)
            nc.scalar.activation(std[:, :], mv[:, :, 1], ACT.Sqrt, bias=eps_col[:, 0:1]).then_inc(std_done, 1)
            for c in range(NCH):
                act.wait_ge(xt_ready, c + 1)
                nc.scalar.activation(xT32[:, TOK * c:TOK * c + TOK], DB[c % 2][:, :], ACT.Copy).then_inc(xt_out, 1)
            act.wait_ge(logit_done, 1)
            nc.scalar.activation(pr[:, :, :], logit[:, :, :], ACT.Sigmoid).then_inc(pr_done, 1)

            def chunk(c):
                for u in range(UNITS):
                    act.wait_ge(up_ready, c * UNITS + u + 1)
                    if u >= 3 or not isinstance(c, int) or c > 0:
                        act.wait_ge(hid_done, c * UNITS + u - 2)
                    nc.scalar.activation(sg[u % 3][:, :], GB[u % 3][:, :], ACT.Silu).then_inc(silu_done, 1)

            chunk(0)
            with act.Fori(1, NCH, 1) as c:
                chunk(c)
            act.wait_ge(mv2_done, TILES)
            nc.scalar.activation(std2[:, :], mv2[:, :, 1], ACT.Sqrt, bias=eps_col[:, 0:1]).then_inc(std2_done, 1)

        @block.vector
        def _(dve):
            for t in range(TILES):
                nc.vector.bn_stats(stats[:, t, :], R[:, t, :]).then_inc(st1, 1)
            for t in range(TILES):
                dve.wait_ge(st1, t + 1)
                nc.vector.bn_aggr(mv[:, t, :], stats[:, t, :]).then_inc(mv_done, 1)
            dve.wait_ge(moe_weights_in, 16 * 5)
            nc.vector.tensor_copy(wuph[:, 0, :, :], wup32[:, 0, :, :]).then_inc(w_split, 1)
            nc.vector.tensor_copy(wuph[:, 1, :, :], wup32[:, 1, :, :]).then_inc(w_split, 1)
            nc.vector.tensor_copy(wrh[:, :], wr32[:, :]).then_inc(w_split, 1)
            dve.wait_ge(std_done, 1)
            nc.vector.reciprocal(rstd[:, :], std[:, :]).then_inc(rstd_done, 1)
            dve.wait_ge(rstd_done, 1)
            for t in range(TILES):
                nc.vector.tensor_scalar(R[:, t, :], R[:, t, :], mv[:, t, 0:1], rstd[:, t:t + 1], ALU.subtract,
                                        ALU.mult).then_inc(ln_done, 1)
            dve.wait_ge(w_split, 3)
            nc.vector.tensor_tensor(wupl[:, 0, :, :], wup32[:, 0, :, :], wuph[:, 0, :, :], ALU.subtract).then_inc(w_split, 1)
            nc.vector.tensor_tensor(wupl[:, 1, :, :], wup32[:, 1, :, :], wuph[:, 1, :, :], ALU.subtract).then_inc(w_split, 1)
            nc.vector.tensor_tensor(wrl[:, :], wr32[:, :], wrh[:, :], ALU.subtract).then_inc(w_split, 1)
            for c in range(NCH):
                dve.wait_ge(xt_out, c + 1)
                cols = slice(TOK * c, TOK * c + TOK)
                nc.vector.tensor_copy(xTh[:, cols], xT32[:, cols]).then_inc(xh_done, 1)
                dve.wait_ge(xh_done, c + 1)
                nc.vector.tensor_tensor(xTl[:, cols], xT32[:, cols], xTh[:, cols], ALU.subtract).then_inc(xl_done, 1)
            nc.vector.memset(cw[:, :, 0:1], 1.0).then_inc(rank_steps, 1)
            dve.wait_ge(logit_ready, 1)
            nc.vector.tensor_tensor(logit[:, :, :], GB[2][:, 0:TILES * E].rearrange("p (t e) -> p t e", e=E),
                                    rb_bc[:, :].unsqueeze(1).broadcast_to([P, TILES, E]), ALU.add).then_inc(logit_done, 1)
            dve.wait_ge(pr_done, 1)
            mine = pr[:, :, :].unsqueeze(3).broadcast_to([P, TILES, E, E])
            other = pr[:, :, :].unsqueeze(2).broadcast_to([P, TILES, E, E])
            nc.vector.tensor_tensor(gt[:, :, :, :], other, mine, ALU.is_gt).then_inc(rank_steps, 1)
            nc.vector.tensor_tensor(eq[:, :, :, :], other, mine, ALU.is_equal).then_inc(rank_steps, 1)
            dve.wait_ge(rank_steps, 3)
            nc.vector.tensor_tensor(eq[:, :, :, :], eq[:, :, :, :], tri[:, :, :].unsqueeze(1).broadcast_to([P, TILES, E, E]),
                                    ALU.mult).then_inc(rank_steps, 1)
            dve.wait_ge(rank_steps, 4)
            nc.vector.tensor_tensor(gt[:, :, :, :], gt[:, :, :, :], eq[:, :, :, :], ALU.add).then_inc(rank_steps, 1)
            dve.wait_ge(rank_steps, 5)
            nc.vector.tensor_reduce(rank[:, :, :], gt[:, :, :, :], AX.X, ALU.add).then_inc(rank_steps, 1)
            dve.wait_ge(rank_steps, 6)
            nc.vector.scalar_tensor_tensor(out=cw[:, :, 1:E1], in0=rank[:, :, :], scalar=1.5, in1=pr[:, :, :],
                                           op0=ALU.is_lt, op1=ALU.mult).then_inc(cw_done, 1)
            dve.wait_ge(cw_done, 1)

            def hidden(c, u):
                dve.wait_ge(silu_done, c * UNITS + u + 1)
                if u >= 6 or not isinstance(c, int) or c > 0:
                    dve.wait_ge(down_ready, c * E1 + (u - 6) // 2 + 1)
                nc.vector.tensor_tensor(hid[u % 6][:, :], sg[u % 3][:, :], UB[u % 3][:, :], ALU.mult).then_inc(hid_done, 1)

            def add(c, e, par):
                dve.wait_ge(down_ready, c * E1 + e + 1)
                if not (isinstance(c, int) and c == 0 and e == 0):
                    dve.wait_ge(acc_done, (c * E1 + e) * CH)
                for i in range(CH):
                    t = c * CH + i
                    nc.vector.scalar_tensor_tensor(out=R[:, bass.ds(t, 1), :], in0=DB[(e + par) % 2][:, P * i:P * i + P].unsqueeze(1),
                                                   scalar=cw[:, bass.ds(t, 1), e],
                                                   in1=R[:, bass.ds(t, 1), :], op0=ALU.mult, op1=ALU.add).then_inc(acc_done, 1)

            def chunk(c, par):
                for e in range(E1):
                    hidden(c, 2 * e)
                    hidden(c, 2 * e + 1)
                    if e:
                        add(c, e - 1, par)
                add(c, E1 - 1, par)
                dve.wait_ge(acc_done, (c * E1 + E1) * CH)
                for i in range(CH):
                    t = c * CH + i
                    nc.vector.bn_stats(stats[:, bass.ds(t, 1), :].rearrange("p o s -> p (o s)"), R[:, bass.ds(t, 1), :].rearrange("p o c -> p (o c)")).then_inc(st2, 1)

            chunk(0, 0)
            chunk(1, 1)
            with dve.Fori(1, NCH // 2, 1) as i:
                chunk(i * 2, 0)
                chunk(i * 2 + 1, 1)
            dve.wait_ge(st2, TILES)
            for t in range(TILES):
                nc.vector.bn_aggr(mv2[:, t, :], stats[:, t, :]).then_inc(mv2_done, 1)
            dve.wait_ge(std2_done, 1)
            nc.vector.reciprocal(rstd2[:, :], std2[:, :]).then_inc(rstd2_done, 1)
            dve.wait_ge(rstd2_done, 1)
            for t in range(TILES):
                nc.vector.tensor_scalar(R[:, t, :], R[:, t, :], mv2[:, t, 0:1], rstd2[:, t:t + 1], ALU.subtract,
                                        ALU.mult).then_inc(fin_done, 1)


def kernel(L0_attn_x, L0_attn_Wattn, L0_attn_battn, L0_attn_Wproj, L0_attn_bproj, L0_attn_embk,
           L0_attn_embv, L0_ffn_Wg_s, L0_ffn_Wu_s, L0_ffn_Wd_s, L0_ffn_Wg, L0_ffn_Wu, L0_ffn_Wd,
           L0_ffn_Wr, L0_ffn_rb):
    import ml_dtypes
    import numpy as np
    import concourse.bacc as bacc
    from concourse.bass_utils import run_bass_kernel_spmd

    f = lambda a: np.ascontiguousarray(np.asarray(a))
    x = f(L0_attn_x)
    B, T, C = x.shape
    E = L0_ffn_Wr.shape[0]
    bqkv = f(L0_attn_battn)
    last = L0_attn_embk.shape[0] - 1
    far = np.clip(T - 1 - np.arange(T + 15), 0, last)
    far_v = np.clip(T - 1 - np.arange(T + 127), 0, last)
    gates = np.concatenate([f(L0_ffn_Wg_s)[None], f(L0_ffn_Wg)], 0)
    ups = np.concatenate([f(L0_ffn_Wu_s)[None], f(L0_ffn_Wu)], 0)
    downs = np.concatenate([f(L0_ffn_Wd_s)[None], f(L0_ffn_Wd)], 0)
    wup = np.stack([gates, ups], 0).transpose(3, 0, 1, 2)
    wdn = downs.reshape(E + 1, C, -1, 128).transpose(3, 0, 2, 1)
    p = np.arange(128)
    m8 = (p[None, :] % 8 == (p[:, None] // 8) % 8).astype(np.float16)
    mh = (p[None, :] // 8 == p[:, None] // 8).astype(np.float16)
    sel8 = (p[:, None] == p[None, :] % 8).astype(ml_dtypes.bfloat16)
    u = np.arange(24) - 8
    causal = np.where((u[None, :] > p[:, None]) & (p[:, None] < 8), -1e30, 0.0).astype(ml_dtypes.bfloat16)
    tri = np.broadcast_to(np.tril(np.ones((E, E), np.float32), -1).reshape(1, -1), (128, E * E))
    arrays = {
        "x": x, "xT": f(x.reshape(B * T, C).T), "Wqkv": f(L0_attn_Wattn),
        "bq": f(bqkv[0:C].reshape(C, 1)), "bk": f(bqkv[C:2 * C].reshape(C, 1)), "bv": f(bqkv[2 * C:]),
        "Wp": f(L0_attn_Wproj), "bp": f(L0_attn_bproj),
        "ekrev": f(f(L0_attn_embk)[far].T), "evrev": f(f(L0_attn_embv)[far_v]),
        "Wup": f(wup), "Wdn": f(wdn), "WrT": f(f(L0_ffn_Wr).T), "rb": f(L0_ffn_rb),
        "ident": np.eye(128, dtype=np.float32), "m8": m8, "mh": mh, "sel8": f(sel8), "causal": causal, "tri": f(tri),
    }
    nc = bacc.Bacc("TRN2", target_bir_lowering=False, num_devices=1)
    args = [nc.dram_tensor(f"in_{k}", a.shape, mybir.dt.from_np(a.dtype), kind="ExternalInput").ap()
            for k, a in arrays.items()]
    out = nc.dram_tensor("out_0", x.shape, F32, kind="ExternalOutput").ap()
    attention_and_experts(nc, *args, out)
    r = run_bass_kernel_spmd(nc, [{f"in_{k}": a for k, a in arrays.items()}], core_ids=[0])
    return r.results[0]["out_0"]
```

```python
from contextlib import ExitStack

import concourse.bass as bass
from concourse import mybir

ALU = mybir.AluOpType
ACT = mybir.ActivationFunctionType
AX = mybir.AxisListType
F32 = mybir.dt.float32
F16 = mybir.dt.float16
BF16 = mybir.dt.bfloat16

P = 128
EPS = 1e-5


def attention_and_experts(nc, x, xT, Wqkv, bq, bk, bv, Wp, bp, ekrev, evrev, Wup, Wdn, WrT, rb,
                          ident_in, m8_in, mh_in, sel8_in, causal_in, tri_in, out):
    B, T, C = x.shape
    H = 16
    D = C // H
    REL = T - P
    G = T // 8
    PAIRS = G // 2
    SCALE = 1.0 / float(D) ** 0.5
    E1 = Wup.shape[2]
    E = E1 - 1
    I = Wup.shape[3]
    TILES = B * T // P
    assert C == P and T == 2 * P and D == 8 and I == 2 * P and REL == P

    outer = ExitStack()
    with outer:
        def sem(name):
            return outer.enter_context(nc.semaphore(name))

        def keep(name, shape, dt):
            return outer.enter_context(nc.sbuf_tensor(name, shape, dt))

        R = keep("R", [P, TILES, C], F32)
        xTh = keep("xTh", [P, TILES * P], F16)
        xTl = keep("xTl", [P, TILES * P], F16)
        wuph = keep("wuph", [P, 2, E1, I], F16)
        wupl = keep("wupl", [P, 2, E1, I], F16)
        wrh = keep("wrh", [P, E], F16)
        wrl = keep("wrl", [P, E], F16)
        rb_bc = keep("rb_bc", [P, E], F32)
        ident = keep("ident", [P, P], F32)
        tri = keep("tri", [P, E, E], F32)

        moe_weights_in = sem("moe_weights_in")
        w_split = sem("w_split")
        const_in = sem("const_in")

        att = ExitStack()
        with att:
            def sb(name, shape, dt):
                return att.enter_context(nc.sbuf_tensor(name, shape, dt))

            wup32 = R[:, TILES - E1 * I // C:TILES, :].rearrange("p (e k) c -> p e (k c)", e=E1)
            wr32 = sb("wr32", [P, E], F32)
            wqkv = sb("wqkv", [P, 3 * C], F32)
            wp = sb("wp", [P, C], F32)
            bq_col = sb("bq_col", [P, 1], F32)
            bk_col = sb("bk_col", [P, 1], F32)
            bks_col = sb("bks_col", [P, 1], F32)
            bv_bc = sb("bv_bc", [P, C], F32)
            bp_bc = sb("bp_bc", [P, C], F32)
            m8 = sb("m8", [P, P], F16)
            mh = sb("mh", [P, P], F16)
            sel8 = sb("sel8", [P, P], BF16)
            causal = sb("causal", [P, 24], BF16)
            ESW = T + 8
            ek32 = sb("ek32", [P, ESW], F32)
            ekh = sb("ekh", [P, ESW], F16)
            ekl = sb("ekl", [P, ESW], F16)
            evw = sb("evw", [P, 2, 16, 8, D], F32)
            xTb = [sb(f"xTb{i}", [P, T], F32) for i in range(2)]
            xb = sb("xb", [P, 2, C], F32)
            qs = sb("qs", [P, 2, T], F16)
            qbd = [sb(f"qbd{i}", [P, 2, G, P], F16) for i in range(2)]
            q2rep = sb("q2rep", [P, H, T], F16)
            q2 = [sb(f"q2_{i}", [P, G, P], F16) for i in range(2)]
            kf = sb("kf", [P, T], F32)
            khi = [sb(f"khi{i}", [P, T], F16) for i in range(2)]
            klo = [sb(f"klo{i}", [P, T], F16) for i in range(2)]
            v1 = [sb(f"v1_{i}", [P, 2, H, 32], F32) for i in range(2)]
            nmax = sb("nmax", [P, G], F32)
            WB = [P * (g // (G // 2) + 1) for g in range(G)]
            PB = [sum(WB[:g]) for g in range(G)]
            prob = sb("prob", [P, sum(WB)], F32)
            pt0 = sb("pt0", [P, G * P], F32)
            pt1 = sb("pt1", [P, G * P // 2], F32)
            z1 = sb("z1", [P, H // 4, T], F32)
            z2 = sb("z2", [P, H, 8, 16], F32)
            ev = z2[:, :, :, :].rearrange("p h t j -> p (h t j)").rearrange("p (y d) -> p y d", d=D)
            yT1 = sb("yT1", [P, T], F32)
            yT2 = sb("yT2", [P, T], F32)
            den = sb("den", [P, T], F32)
            ysum = sb("ysum", [P, T], F32)
            rden = sb("rden", [P, T], F32)
            yT = sb("yT", [P, T], F32)
            xpb = sb("xpb", [P, 2, C], F32)
            rt = sb("rt", [P, 2, C], F32)
            lnst = sb("lnst", [P, 2, 6], F32)
            lnmv = sb("lnmv", [P, 2, 2], F32)
            lntmp = sb("lntmp", [P, 4, 2], F32)

            S = [att.enter_context(nc.psum_tensor(f"S{i}", [P, 512], F32)) for i in range(4)]
            TB = [att.enter_context(nc.psum_tensor(f"TB{i}", [P, 512], F32)) for i in range(3)]
            XB = att.enter_context(nc.psum_tensor("XB", [P, 512], F32))

            qd = [nc.dram_tensor(f"qd{i}", [2, D, H, T], F16, kind="Internal").ap() for i in range(2)]
            y1d = [nc.dram_tensor(f"y1d{i}", [H, 2 * D, T], F32, kind="Internal").ap() for i in range(2)]
            y2d = [nc.dram_tensor(f"y2d{i}", [H, D, T], F32, kind="Internal").ap() for i in range(2)]

            early_in = sem("early_in")
            zeroed = sem("zeroed")
            ek_ready = sem("ek_ready")
            bks_ready = sem("bks_ready")
            xT_in = [sem("xT_in0"), sem("xT_in1")]
            xb_in = sem("xb_in")
            qk_ready = sem("qk_ready")
            hi_done = sem("hi_done")
            qlo_done = sem("qlo_done")
            kf_done = sem("kf_done")
            klo_done = sem("klo_done")
            v_ready = sem("v_ready")
            v_done = sem("v_done")
            qbd_done = sem("qbd_done")
            evw_ready = sem("evw_ready")
            q_spill = sem("q_spill")
            q2rep_in = sem("q2rep_in")
            q2_done = sem("q2_done")
            score_ready = sem("score_ready")
            max_done = sem("max_done")
            exp_done = sem("exp_done")
            tr_ready = sem("tr_ready")
            tr_out_a = sem("tr_out_a")
            tr_out_v = sem("tr_out_v")
            y_ready = sem("y_ready")
            y_out_a = sem("y_out_a")
            y_out_v = sem("y_out_v")
            y_spill = sem("y_spill")
            y_back = sem("y_back")
            ysum_done = sem("ysum_done")
            rden_done = sem("rden_done")
            qbdl_done = sem("qbdl_done")
            st_done = sem("st_done")
            ln_chain = sem("ln_chain")
            x1_done = sem("x1_done")
            xturn_ready = sem("xturn_ready")
            xh_done = sem("xh_done")
            xl_done = sem("xl_done")
            wup_in = sem("wup_in")
            yT_done = sem("yT_done")
            xpb_done = sem("xpb_done")
            proj_ready = sem("proj_ready")
            r_done = sem("r_done")

            ORDER = [15, 14, 13, 12, 11, 10, 1, 0, 9, 8, 3, 2, 7, 6, 5, 4]
            assert sorted(ORDER) == list(range(PAIRS))

            def bank(o, par):
                return S[(o + 2 * par) % 4]

            GROUPS = [(28, 1), (28, 0), (24, 1), (24, 0), (20, 1), (20, 0), (0, 0), (16, 1), (16, 0), (4, 0), (12, 0),
                      (8, 0)]
            SLOT = [3, 4, 5, 6, 7, 8, 9, 11, 12, 13, 15, None]
            NG = len(GROUPS)
            PT1_LAST = 7
            BY_ACT = [1, 3, 5, 6, 8, 10, 11]
            BY_DVE = [k for k in range(NG) if k not in BY_ACT]
            Y_ACT = [0, 2, 4]
            Y_DVE = [1, 3, 5]
            PIECES = 4
            GP = G // PIECES
            Y_SPILLS = 4 + 16

            def count(k, ks):
                return sum(1 for j in ks if j <= k)

            def y_out_wait(eng, n, k):
                if k in Y_ACT:
                    eng.wait_ge(y_out_a, n * len(Y_ACT) + count(k, Y_ACT))
                else:
                    eng.wait_ge(y_out_v, n * len(Y_DVE) + count(k, Y_DVE))

            def group_out_wait(eng, n, k):
                if k in BY_ACT:
                    eng.wait_ge(tr_out_a, n * len(BY_ACT) + count(k, BY_ACT))
                else:
                    eng.wait_ge(tr_out_v, n * len(BY_DVE) + count(k, BY_DVE))

            block = att.enter_context(nc.Block())

            @block.sync
            def _(sp):
                def load_xT(m, par):
                    sp.dma_start(xTb[par][:, :], xT[:, bass.ds(m * T, T)]).then_inc(xT_in[par], 16)

                def load_xb(n):
                    sp.dma_start(xb[:, :, :], x[bass.ds(n, 1), :, :].rearrange(
                        "o (i p) c -> p (o i) c", p=P)).then_inc(xb_in, 16)

                def spill_q(m, par):
                    sp.wait_ge(qlo_done, m + 1)
                    for a in range(2):
                        sp.dma_start(qd[par][a].rearrange("d h t -> h d t"), qs[:, a, :]).then_inc(q_spill, 16)

                def spread_q(m, par):
                    sp.wait_ge(q_spill, m * 32 + 32)
                    if not (isinstance(m, int) and m == 0):
                        sp.wait_ge(q2_done, m)
                    for a in range(2):
                        src = qd[par][a].rearrange("d h t -> d (h t)")
                        sp.dma_start(q2rep[64 * a:64 * a + 64, :, :].rearrange("p h t -> p (h t)"),
                                     src.unsqueeze(0).broadcast_to([8, D, H * T])).then_inc(q2rep_in, 16)

                def spill_y1(n, par):
                    y_out_wait(sp, n, 0)
                    y_out_wait(sp, n, 1)
                    for hq in range(4):
                        sp.dma_start(y1d[par].rearrange("(j q) r t -> q r j t", q=4)[hq],
                                     z1[32 * hq:32 * hq + 2 * D, :, :]).then_inc(y_spill, 16)

                def spill_y2(n, par, half, rs):
                    if half == 0:
                        y_out_wait(sp, n, Y_ACT[-1])
                        y_out_wait(sp, n, Y_DVE[-1])
                    for r in rs:
                        row, tt = 64 * half + D * r, 7 - r
                        at = P * half + 16 * tt
                        sp.dma_start(y2d[par].rearrange("h d t -> d h t")[:, :, at:at + 16],
                                     z2[row:row + D, :, tt, :]).then_inc(y_spill, 16)

                def back_y(n, par):
                    sp.wait_ge(y_spill, (n + 1) * (16 * Y_SPILLS))
                    sp.wait_ge(yT_done, n + 1)
                    for dst, src in ((yT1, y1d[par][:, 0:D, :]), (den, y1d[par][:, D:2 * D, :]), (yT2, y2d[par])):
                        sp.dma_start(dst[:, :], src).then_inc(y_back, 16)

                def step(n, par, first=False, last=False):
                    if not last:
                        if not first:
                            sp.wait_ge(v_ready, n)
                        load_xT(n + 1, 1 - par)
                    if not first:
                        spill_y2(n - 1, 1 - par, 0, range(8))
                    if not last:
                        spill_q(n + 1, 1 - par)
                    if not first:
                        spill_y2(n - 1, 1 - par, 1, range(4))
                    if not last:
                        spread_q(n + 1, 1 - par)
                    if not first:
                        spill_y2(n - 1, 1 - par, 1, range(4, 8))
                        back_y(n - 1, 1 - par)
                        sp.wait_ge(xpb_done, n)
                    load_xb(n)
                    spill_y1(n, par)

                load_xT(0, 0)
                sp.dma_start(wqkv[:, :], Wqkv).then_inc(early_in, 16)
                sp.dma_start(bq_col[:, :], bq).then_inc(early_in, 16)
                sp.dma_start(bk_col[:, :], bk).then_inc(early_in, 16)
                sp.dma_start(bv_bc[:, :], bv.partition_broadcast(P)).then_inc(early_in, 16)
                spill_q(0, 0)
                spread_q(0, 0)
                step(0, 0, first=True)
                with sp.Fori(0, B // 2 - 1, 1) as i:
                    step(i * 2 + 1, 1)
                    step(i * 2 + 2, 0)
                step(B - 1, 1, last=True)
                spill_y2(B - 1, 1, 0, range(8))
                spill_y2(B - 1, 1, 1, range(8))
                back_y(B - 1, 1)

            @block.gpsimd
            def _(pool):
                for dst, src in ((m8, m8_in), (mh, mh_in), (sel8, sel8_in), (causal, causal_in), (ident, ident_in),
                                 (wp, Wp)):
                    pool.dma_start(dst[:, :], src).then_inc(const_in, 16)
                for a in range(2):
                    for t in range(8):
                        r = 64 * a + D * t
                        pool.dma_start(ek32[r:r + D, :], ekrev[:, 7 - t:7 - t + ESW]).then_inc(const_in, 16)
                pool.dma_start(z2[:, :, :, :].rearrange("p h t j -> p (h t j)"),
                               bass.AP(evrev.tensor, evrev.offset, [[D, P], [1, T * D]])).then_inc(const_in, 16)
                pool.dma_start(bp_bc[:, :], bp.partition_broadcast(P)).then_inc(const_in, 16)
                pool.dma_start(wup32, Wup[:, 0, :, :]).then_inc(wup_in, 16)
                pool.dma_start(wr32[:, :], WrT).then_inc(moe_weights_in, 16)
                pool.dma_start(rb_bc[:, :], rb.partition_broadcast(P)).then_inc(moe_weights_in, 16)
                pool.dma_start(tri[:, :, :].rearrange("p a b -> p (a b)"), tri_in).then_inc(moe_weights_in, 16)
                nc.gpsimd.memset(prob[:, :], 0.0).then_inc(zeroed, 1)
                pool.wait_ge(const_in, CONSTS)

                def mask_q_lo(m, par):
                    pool.wait_ge(qlo_done, m + 1)
                    nc.gpsimd.tensor_tensor(qbd[par][:, 1, :, :].rearrange("p g (h t) -> p g h t", h=H),
                                            qs[:, 1, :].rearrange("p (g t) -> p g t", t=8).unsqueeze(2)
                                            .broadcast_to([P, G, H, 8]),
                                            mh[:, :].rearrange("p (h t) -> p h t", h=H).unsqueeze(1)
                                            .broadcast_to([P, G, H, 8]), ALU.mult).then_inc(qbdl_done, 1)

                def residual(n):
                    pool.wait_ge(xb_in, n * 16 + 16)
                    pool.wait_ge(r_done, n + 1)
                    nc.gpsimd.tensor_tensor(xpb[:, :, :], xb[:, :, :], bp_bc[:, :].unsqueeze(1).broadcast_to([P, 2, C]),
                                            ALU.add).then_inc(xpb_done, 1)

                mask_q_lo(0, 0)
                mask_q_lo(1, 1)
                residual(0)
                for w in range(2):
                    pool.wait_ge(wup_in, 16 * (w + 1))
                    nc.gpsimd.tensor_copy(wuph[:, w, :, :], wup32).then_inc(w_split, 1)
                    pool.wait_ge(w_split, 2 * w + 1)
                    nc.gpsimd.tensor_tensor(wupl[:, w, :, :], wup32, wuph[:, w, :, :], ALU.subtract).then_inc(w_split, 1)
                    if w == 0:
                        pool.wait_ge(w_split, 2)
                        pool.dma_start(wup32, Wup[:, 1, :, :]).then_inc(wup_in, 16)
                        mask_q_lo(2, 0)
                        residual(1)
                pool.wait_ge(moe_weights_in, 16 * 3)
                nc.gpsimd.tensor_copy(wrh[:, :], wr32[:, :]).then_inc(w_split, 1)
                pool.wait_ge(w_split, 5)
                nc.gpsimd.tensor_tensor(wrl[:, :], wr32[:, :], wrh[:, :], ALU.subtract).then_inc(w_split, 1)
                with pool.Fori(0, B // 2 - 2, 1) as i:
                    mask_q_lo(i * 2 + 3, 1)
                    residual(i * 2 + 2)
                    mask_q_lo(i * 2 + 4, 0)
                    residual(i * 2 + 3)
                mask_q_lo(B - 1, 1)
                residual(B - 2)
                residual(B - 1)

            @block.tensor
            def _(pe):
                def project_qk(m, par, halfm):
                    pe.wait_ge(xT_in[par], halfm * 16 + 16)
                    if not (isinstance(m, int) and m < 2):
                        pe.wait_ge(xl_done, m - 1)
                    nc.tensor.matmul(XB[:, 0:T], wqkv[:, 0:C], xTb[par][:, :], start=True, stop=True)
                    nc.tensor.matmul(XB[:, T:2 * T], wqkv[:, C:2 * C], xTb[par][:, :], start=True,
                                     stop=True).then_inc(qk_ready, 1)

                def project_v(m, par):
                    pe.wait_ge(kf_done, m + 1)
                    nc.tensor.matmul(XB[:, 0:C], xTb[par][:, 0:P], wqkv[:, 2 * C:3 * C], start=True, stop=True)
                    nc.tensor.matmul(XB[:, C:2 * C], xTb[par][:, P:T], wqkv[:, 2 * C:3 * C], start=True,
                                     stop=True).then_inc(v_ready, 1)

                def project_out(n, m):
                    pe.wait_ge(yT_done, n + 2)
                    pe.wait_ge(v_done, m)
                    pe.wait_ge(xl_done, n + 1)
                    nc.tensor.matmul(XB[:, 0:C], yT[:, 0:P], wp[:, :], start=True, stop=True)
                    nc.tensor.matmul(XB[:, C:2 * C], yT[:, P:T], wp[:, :], start=True,
                                     stop=True).then_inc(proj_ready, 1)

                def turn_rows(n):
                    pe.wait_ge(x1_done, n + 1)
                    for i in range(2):
                        last = nc.tensor.transpose(XB[:, P * i:P * i + P], rt[:, i, :], ident[:, :])
                    last.then_inc(xturn_ready, 1)

                def scores(n, par, o, first):
                    j = ORDER[o]
                    if o >= 4:
                        pe.wait_ge(exp_done, n * PAIRS + o - 3)
                    elif not first:
                        y_out_wait(pe, n - 1, o + 2)
                    W2 = 16 * (j + 1)
                    for a in range(2):
                        g = 2 * j + a
                        out_ = bank(o, par)[:, 256 * a:256 * a + W2]
                        qh = qbd[par][:, 0, g, :]
                        ql = qbd[par][:, 1, g, :]
                        qr = q2[par][:, g, :]
                        off = T - 8 - 8 * g
                        nc.tensor.matmul(out_, qh, khi[par][:, 0:W2], start=(a == 0), stop=False, skip_group_check=True)
                        nc.tensor.matmul(out_, qh, klo[par][:, 0:W2], start=False, stop=False, skip_group_check=True)
                        nc.tensor.matmul(out_, ql, khi[par][:, 0:W2], start=False, stop=False, skip_group_check=True)
                        nc.tensor.matmul(out_, qr, ekh[:, off:off + W2], start=False, stop=False, skip_group_check=True)
                        nc.tensor.matmul(out_, qr, ekl[:, off:off + W2], start=False, stop=False, skip_group_check=True)
                        last = nc.tensor.matmul(out_[:, W2 - 16:W2], sel8[:, :], causal[:, 8 - 8 * a:24 - 8 * a],
                                                start=False, stop=True, skip_group_check=True)
                    last.then_inc(score_ready, 1)

                def turn(n, k):
                    g0, blk = GROUPS[k]
                    done = 1 + max(ORDER.index(g0 // 2), ORDER.index(g0 // 2 + 1))
                    pe.wait_ge(exp_done, n * PAIRS + done)
                    if k >= 3:
                        group_out_wait(pe, n, k - 3)
                    for i in range(4):
                        at = PB[g0 + i] + P * blk
                        last = nc.tensor.transpose(TB[k % 3][:, P * i:P * i + P], prob[:, at:at + P],
                                                   ident[:, :])
                    last.then_inc(tr_ready, 1)

                def content(n, par, k, blk):
                    group_out_wait(pe, n, PT1_LAST)
                    if blk == 0:
                        group_out_wait(pe, n, BY_ACT[-1])
                        group_out_wait(pe, n, BY_DVE[-1])
                    src = (pt1 if blk else pt0)[:, :].rearrange("p (g h t) -> p g h t", h=H, t=8)
                    for jj in range(2):
                        for hq in range(4):
                            h = 4 * (2 * k + jj) + hq
                            o = bank(k, par)[32 * hq:32 * hq + 32, T * jj + P * blk:T * jj + T]
                            last = nc.tensor.matmul(o, v1[par][:, blk, h, :], src[:, :, h, :],
                                                    start=(jj == 0 and blk == 1), stop=(blk == 0),
                                                    skip_group_check=True, tile_position=(0, 32 * hq))
                    if blk == 0:
                        last.then_inc(y_ready, 1)

                def relative(n, par, loads):
                    p0 = pt0[:, :].rearrange("p (b tt a h t) -> p b tt a h t", b=2, a=2, h=H, t=8)
                    p1 = pt1[:, :].rearrange("p (tt a h t) -> p tt a h t", a=2, h=H, t=8)
                    for k in loads:
                        if k >= 4:
                            y_out_wait(pe, n, k - 4)
                        for jj in range(4):
                            j = 4 * (k - 2) + jj
                            for half, blk in ((0, 0), (1, 0), (1, 1)):
                                lhs = evw[:, 1 - (half - blk), 15 - j, :, :].rearrange("p r d -> p (r d)")
                                src = p1[:, :, j // 8, :, j % 8] if blk else p0[:, half, :, j // 8, :, j % 8]
                                last = nc.tensor.matmul(bank(k, par)[64 * half:64 * half + 64, P * jj:P * jj + P], lhs, src,
                                                        start=(jj == 0 and blk == 0), stop=(half == blk),
                                                        skip_group_check=True, tile_position=(0, 64 * half))
                        last.then_inc(y_ready, 1)

                def step(n, par, halfm, first=False, last=False):
                    pe.wait_ge(qbd_done, n + 1)
                    pe.wait_ge(qbdl_done, n + 1)
                    pe.wait_ge(klo_done, n + 1)
                    pe.wait_ge(q2_done, n + 1)
                    pe.wait_ge(v_done, n + 1)
                    for o in range(PAIRS):
                        scores(n, par, o, first)
                        if o == 2 and not last:
                            project_qk(n + 1, 1 - par, halfm)
                        for k in range(NG):
                            if SLOT[k] == o:
                                turn(n, k)
                    content(n, par, 0, 1)
                    turn(n, NG - 1)
                    content(n, par, 1, 1)
                    if not last:
                        project_v(n + 1, 1 - par)
                    content(n, par, 0, 0)
                    content(n, par, 1, 0)
                    if not first:
                        project_out(n - 1, n + 1 if last else n + 2)
                    relative(n, par, range(2, 6))
                    if not first:
                        turn_rows(n - 1)

                pe.wait_ge(early_in, 64)
                project_qk(0, 0, 0)
                project_v(0, 0)
                pe.wait_ge(const_in, CONSTS)
                pe.wait_ge(ek_ready, 2)
                pe.wait_ge(evw_ready, 2)
                pe.wait_ge(zeroed, ZEROS)
                step(0, 0, 0, first=True)
                with pe.Fori(0, B // 2 - 1, 1) as i:
                    step(i * 2 + 1, 1, i + 1)
                    step(i * 2 + 2, 0, i + 1)
                step(B - 1, 1, 0, last=True)
                project_out(B - 1, B)
                turn_rows(B - 1)

            @block.scalar
            def _(act):
                def split_hi(m, par):
                    act.wait_ge(qk_ready, m + 1)
                    if not (isinstance(m, int) and m == 0):
                        act.wait_ge(qbd_done, m)
                        act.wait_ge(q_spill, m * 32)
                    nc.scalar.activation(qs[:, 0, :], XB[:, 0:T], ACT.Identity, bias=bq_col[:, 0:1])
                    nc.scalar.activation(khi[par][:, :], XB[:, T:2 * T], ACT.Identity, bias=bks_col[:, 0:1],
                                         scale=SCALE).then_inc(hi_done, 1)

                def exps(n, par, o):
                    j = ORDER[o]
                    act.wait_ge(max_done, n * PAIRS + o + 1)
                    W2 = 16 * (j + 1)
                    for a in range(2):
                        g = 2 * j + a
                        last = nc.scalar.activation(prob[:, PB[g]:PB[g] + W2], bank(o, par)[:, 256 * a:256 * a + W2],
                                                    ACT.Exp, bias=nmax[:, g:g + 1])
                    last.then_inc(exp_done, 1)

                def turned(n, k):
                    g0, blk = GROUPS[k]
                    act.wait_ge(tr_ready, n * NG + k + 1)
                    dst = pt1[:, P * (g0 - G // 2):P * (g0 - G // 2) + 512] if blk else pt0[:, P * g0:P * g0 + 512]
                    nc.scalar.activation(dst, TB[k % 3][:, :], ACT.Copy).then_inc(tr_out_a, 1)

                def step(n, par, first=False, last=False):
                    for o in range(PAIRS):
                        exps(n, par, o)
                        if o == 2 and not last:
                            split_hi(n + 1, 1 - par)
                        for k in BY_ACT:
                            if SLOT[k] == o:
                                turned(n, k)
                    turned(n, NG - 1)
                    if not first:
                        act.wait_ge(y_spill, n * (16 * Y_SPILLS))
                    for k in Y_ACT:
                        act.wait_ge(y_ready, n * 6 + k + 1)
                        if k == 0:
                            nc.scalar.activation(z1[:, 0:2, :], bank(0, par)[:, :], ACT.Copy).then_inc(y_out_a, 1)
                        else:
                            j0 = 4 * (k - 2)
                            nc.scalar.activation(z2[:, :, :, j0:j0 + 4].rearrange("p h t j -> p j t h"),
                                                 bank(k, par)[:, :].rearrange("p (j t h) -> p j t h", j=4, t=8),
                                                 ACT.Copy).then_inc(y_out_a, 1)
                    if not first:
                        rows_hi(n - 1)

                def rows_hi(n):
                    act.wait_ge(xturn_ready, n + 1)
                    nc.scalar.activation(xTh[:, bass.ds(n * T, T)], XB[:, 0:T], ACT.Copy).then_inc(xh_done, 1)

                act.wait_ge(early_in, 64)
                act.wait_ge(bks_ready, 1)
                split_hi(0, 0)
                act.wait_ge(zeroed, ZEROS)
                step(0, 0, first=True)
                with act.Fori(0, B // 2 - 1, 1) as i:
                    step(i * 2 + 1, 1)
                    step(i * 2 + 2, 0)
                step(B - 1, 1, last=True)
                rows_hi(B - 1)

            @block.vector
            def _(dve):
                def split_lo(m, par):
                    dve.wait_ge(hi_done, m + 1)
                    if not (isinstance(m, int) and m == 0):
                        dve.wait_ge(qbdl_done, m)
                    nc.vector.scalar_tensor_tensor(out=qs[:, 1, :], in0=XB[:, 0:T], scalar=bq_col[:, 0:1],
                                                   in1=qs[:, 0, :], op0=ALU.add, op1=ALU.subtract).then_inc(qlo_done, 1)
                    if not (isinstance(m, int) and m == 0):
                        dve.wait_ge(klo_done, m)
                    nc.vector.tensor_scalar(kf[:, :], XB[:, T:2 * T], bk_col[:, 0:1], SCALE, ALU.add,
                                            ALU.mult).then_inc(kf_done, 1)
                    dve.wait_ge(kf_done, m + 1)
                    nc.vector.tensor_tensor(klo[par][:, :], kf[:, :], khi[par][:, :],
                                            ALU.subtract).then_inc(klo_done, 1)

                def take_v(m, par):
                    dve.wait_ge(v_ready, m + 1)
                    nc.vector.tensor_tensor(v1[par][:, :, :, 0:D],
                                            XB[:, 0:2 * C].rearrange("p (b h d) -> p b h d", b=2, h=H),
                                            bv_bc[:, :].rearrange("p (h d) -> p h d", h=H).unsqueeze(1)
                                            .broadcast_to([P, 2, H, D]), ALU.add).then_inc(v_done, 1)

                def mask_q2(m, par, p):
                    dve.wait_ge(q2rep_in, (m + 1) * 32)
                    ins = nc.vector.tensor_tensor(q2[par][:, p * GP:p * GP + GP, :].rearrange("p g (h t) -> p g h t", h=H),
                                            q2rep[:, :, 8 * p * GP:8 * (p + 1) * GP].rearrange("p h (g t) -> p g h t", t=8),
                                            m8[:, :].rearrange("p (h t) -> p h t", h=H).unsqueeze(1)
                                            .broadcast_to([P, GP, H, 8]), ALU.mult)
                    if p == PIECES - 1:
                        ins.then_inc(q2_done, 1)

                def mask_q(m, par, p):
                    ins = nc.vector.tensor_tensor(qbd[par][:, 0, p * GP:p * GP + GP, :].rearrange("p g (h t) -> p g h t", h=H),
                                            qs[:, 0, 8 * p * GP:8 * (p + 1) * GP].rearrange("p (g t) -> p g t", t=8)
                                            .unsqueeze(2).broadcast_to([P, GP, H, 8]),
                                            mh[:, :].rearrange("p (h t) -> p h t", h=H).unsqueeze(1)
                                            .broadcast_to([P, GP, H, 8]), ALU.mult)
                    if p == PIECES - 1:
                        ins.then_inc(qbd_done, 1)

                def maxima(n, par, o):
                    j = ORDER[o]
                    W2 = 16 * (j + 1)
                    dve.wait_ge(score_ready, n * PAIRS + o + 1)
                    nc.vector.tensor_reduce(nmax[:, 2 * j:2 * j + 2],
                                            bank(o, par)[:, :].rearrange("p (a w) -> p a w", a=2)[:, :, 0:W2],
                                            AX.X, ALU.max, negate=True).then_inc(max_done, 1)

                def turned(n, k):
                    g0, blk = GROUPS[k]
                    dve.wait_ge(tr_ready, n * NG + k + 1)
                    dst = pt1[:, P * (g0 - G // 2):P * (g0 - G // 2) + 512] if blk else pt0[:, P * g0:P * g0 + 512]
                    nc.vector.tensor_copy(dst, TB[k % 3][:, :]).then_inc(tr_out_v, 1)

                def invert(n, half):
                    dve.wait_ge(y_back, n * 48 + 48)
                    nc.vector.reciprocal(rden[:, P * half:P * half + P], den[:, P * half:P * half + P]).then_inc(rden_done, 1)

                def normalise(n):
                    nc.vector.tensor_tensor(ysum[:, :], yT1[:, :], yT2[:, :], ALU.add).then_inc(ysum_done, 1)
                    dve.wait_ge(ysum_done, n + 1)
                    dve.wait_ge(rden_done, n * 2 + 2)
                    nc.vector.tensor_tensor(yT[:, :], ysum[:, :], rden[:, :], ALU.mult).then_inc(yT_done, 1)

                def residual(n):
                    dve.wait_ge(proj_ready, n + 1)
                    dve.wait_ge(xpb_done, n + 1)
                    nc.vector.tensor_tensor(rt[:, :, :], XB[:, 0:2 * C].rearrange("p (i c) -> p i c", i=2),
                                            xpb[:, :, :], ALU.add).then_inc(r_done, 1)

                def layer_norm(n):
                    dve.wait_ge(r_done, n + 2)
                    normalise_rows(nc, dve, ln_chain, n * LN_STEPS(2), rt, 2, lnst, lnmv, lntmp)
                    for i in range(2):
                        last = nc.vector.tensor_scalar(rt[:, i, :], rt[:, i, :], lnmv[:, i, 0:1], lntmp[:, 1, i:i + 1],
                                                       ALU.subtract, ALU.mult)
                    last.then_inc(x1_done, 1)

                def keep_rows(n):
                    dve.wait_ge(x1_done, n + 1)
                    dve.wait_ge(w_split, 4)
                    nc.vector.tensor_copy(R[:, bass.ds(n * 2, 2), :], rt[:, :, :]).then_inc(st_done, 1)

                def rows_lo(n):
                    dve.wait_ge(xh_done, n + 1)
                    nc.vector.tensor_tensor(xTl[:, bass.ds(n * T, T)], XB[:, 0:T], xTh[:, bass.ds(n * T, T)],
                                            ALU.subtract).then_inc(xl_done, 1)

                def take_y(n, par, k):
                    dve.wait_ge(y_ready, n * 6 + k + 1)
                    if k == 1:
                        nc.vector.tensor_copy(z1[:, 2:4, :], bank(1, par)[:, :].rearrange("p (j t) -> p j t", j=2)).then_inc(y_out_v, 1)
                    else:
                        j0 = 4 * (k - 2)
                        nc.vector.tensor_copy(z2[:, :, :, j0:j0 + 4].rearrange("p h t j -> p j t h"),
                                              bank(k, par)[:, :].rearrange("p (j t h) -> p j t h", j=4, t=8)).then_inc(y_out_v, 1)

                def step(n, par, first=False, last=False):
                    for o in range(PAIRS):
                        maxima(n, par, o)
                        if o == 3 and not last:
                            split_lo(n + 1, 1 - par)
                        if 4 <= o < 4 + PIECES and not last:
                            mask_q(n + 1, 1 - par, o - 4)
                        if 12 <= o < 12 + PIECES and not last:
                            mask_q2(n + 1, 1 - par, o - 12)
                        for k in BY_DVE:
                            if SLOT[k] == o:
                                turned(n, k)
                    if not first:
                        invert(n - 1, 0)
                    if not last:
                        take_v(n + 1, 1 - par)
                    if not first:
                        invert(n - 1, 1)
                        normalise(n - 1)
                        dve.wait_ge(y_spill, n * (16 * Y_SPILLS))
                    take_y(n, par, 1)
                    if not first:
                        residual(n - 1)
                        layer_norm(n - 1)
                    take_y(n, par, 3)
                    take_y(n, par, 5)
                    if not first:
                        keep_rows(n - 1)
                        rows_lo(n - 1)

                for par in range(2):
                    nc.vector.memset(v1[par][:, :, :, D:32], 1.0).then_inc(zeroed, 1)
                nc.vector.memset(ysum[:, :], 0.0).then_inc(r_done, 1)
                nc.vector.memset(rden[:, :], 0.0).then_inc(xl_done, 1)
                nc.vector.memset(yT[:, :], 0.0).then_inc(yT_done, 1)
                nc.vector.memset(ekl[64:P, :], 0.0).then_inc(zeroed, 1)
                dve.wait_ge(early_in, 64)
                nc.vector.tensor_scalar(bks_col[:, :], bk_col[:, :], SCALE, None, ALU.mult).then_inc(bks_ready, 1)
                split_lo(0, 0)
                take_v(0, 0)
                dve.wait_ge(const_in, CONSTS)
                nc.vector.tensor_copy(ekh[:, :], ek32[:, :]).then_inc(ek_ready, 1)
                dve.wait_ge(ek_ready, 1)
                nc.vector.tensor_tensor(ekl[0:64, :], ek32[0:64, :], ekh[0:64, :], ALU.subtract).then_inc(ek_ready, 1)
                for p in range(PIECES):
                    mask_q(0, 0, p)
                for p in range(PIECES):
                    mask_q2(0, 0, p)
                for b in range(2):
                    nc.vector.tensor_copy(evw[:, b, :, :, :], ev[:, P * b:P * b + P, :].rearrange(
                        "p (r j) d -> p j r d", j=16)).then_inc(evw_ready, 1)
                step(0, 0, first=True)
                with dve.Fori(0, B // 2 - 1, 1) as i:
                    step(i * 2 + 1, 1)
                    step(i * 2 + 2, 0)
                step(B - 1, 1, last=True)
                invert(B - 1, 0)
                invert(B - 1, 1)
                normalise(B - 1)
                residual(B - 1)
                layer_norm(B - 1)
                keep_rows(B - 1)
                rows_lo(B - 1)

        experts(nc, sem, E, E1, I, TILES, R, xTh, xTl, wuph, wupl, Wdn, wrh, wrl, rb_bc, tri, out)


CONSTS = 16 * (6 + 16 + 2)
ZEROS = 1 + 3


def LN_STEPS(rows):
    return 2 * rows + 12


def normalise_rows(nc, dve, chain, base, src, rows, st, mv, tmp):
    done = [0]

    def link(ins):
        done[0] += 1
        ins.then_inc(chain, 1)

    def linked(ins):
        link(ins)
        dve.wait_ge(chain, base + done[0])

    for i in range(rows):
        link(nc.vector.bn_stats(st[:, i, :], src[:, i, :]))
    dve.wait_ge(chain, base + done[0])
    nc.vector.memset(tmp[:, 3, 0:1], 0.0)
    for i in range(rows):
        link(nc.vector.bn_aggr(mv[:, i, :], st[:, i, :]))
    dve.wait_ge(chain, base + done[0])
    ve, r, t = tmp[:, 0, 0:rows], tmp[:, 1, 0:rows], tmp[:, 2, 0:rows]
    I32 = mybir.dt.int32
    linked(nc.vector.tensor_scalar(ve, mv[:, :, 1], EPS, None, ALU.add))
    linked(nc.vector.tensor_scalar(t.bitcast(I32), ve.bitcast(I32), 1, None, ALU.logical_shift_right))
    linked(nc.vector.tensor_scalar(r.bitcast(I32), t.bitcast(I32), -1.0, float(0x5f3759df), ALU.mult, ALU.add))
    for _ in range(3):
        linked(nc.vector.scalar_tensor_tensor(out=t, in0=r, scalar=-0.5, in1=r, op0=ALU.mult, op1=ALU.mult))
        linked(nc.vector.tensor_tensor(t, t, ve, ALU.mult))
        linked(nc.vector.scalar_tensor_tensor(out=r, in0=t, scalar=1.5, in1=r, op0=ALU.add, op1=ALU.mult))
    assert done[0] == LN_STEPS(rows)


def experts(nc, sem, E, E1, I, TILES, R, xTh, xTl, wuph, wupl, Wdn, wrh, wrl, rb_bc, tri, out):
    C = P
    CH = 4
    NCH = TILES // CH
    TOK = CH * P
    ctx = ExitStack()
    with ctx:
        def sb(name, shape, dt):
            return ctx.enter_context(nc.sbuf_tensor(name, shape, dt))

        def ps(name):
            return ctx.enter_context(nc.psum_tensor(name, [P, 512], F32))

        acc = [sb(f"acc{i}", [P, CH, C], F32) for i in range(2)]
        wdn32 = sb("wdn32", [P, E1, 2, C], F32)
        lnst = sb("lnst2", [P, CH, 6], F32)
        lnmv = sb("lnmv2", [P, CH, 2], F32)
        lntmp = sb("lntmp2", [P, 4, CH], F32)
        logit = sb("logit", [P, TILES, E], F32)
        pr = sb("pr", [P, TILES, E], F32)
        gt = sb("gt", [P, TILES, E, E], F32)
        eq = sb("eq", [P, TILES, E, E], F32)
        rank = sb("rank", [P, TILES, E], F32)
        cw = sb("cw", [P, TILES, E1], F32)
        cwc = [sb(f"cwc{i}", [P, CH, E1], F32) for i in range(2)]
        sg = [sb(f"sg{i}", [P, TOK], F32) for i in range(3)]
        hid = [sb(f"hid{i}", [P, TOK], F32) for i in range(6)]

        GB = [ps(f"GB{i}") for i in range(3)]
        UB = [ps(f"UB{i}") for i in range(3)]
        DB = [ps(f"DB{i}") for i in range(2)]

        wdn_in = sem("wdn_in")
        logit_ready = sem("logit_ready")
        logit_done = sem("logit_done")
        pr_done = sem("pr_done")
        rank_steps = sem("rank_steps")
        cw_done = sem("cw_done")
        cwc_done = sem("cwc_done")
        acc_in = sem("acc_in")
        up_ready = sem("up_ready")
        silu_done = sem("silu_done")
        hid_done = sem("hid_done")
        down_ready = sem("down_ready")
        acc_done = sem("acc_done")
        ln_chain = sem("ln_chain2")
        fin_done = sem("fin_done")
        stored = [sem("stored0"), sem("stored1")]

        UNITS = 2 * E1
        SUMS = E1 * CH
        block = ctx.enter_context(nc.Block())

        @block.sync
        def _(sp):
            o = out.rearrange("b (i p) c -> p (b i) c", p=P)
            for a, b in ((0, 1), (1, E1)):
                sp.dma_start(wdn32[:, a:b, :, :], Wdn[:, a:b, :, :]).then_inc(wdn_in, 16)
            with sp.Fori(0, NCH // 2, 1) as i:
                for par in range(2):
                    sp.wait_ge(fin_done, (i * 2 + par + 1) * CH)
                    sp.dma_start(o[:, bass.ds((i * 2 + par) * CH, CH), :], acc[par][:, :, :]).then_inc(stored[par], 16)
            sp.wait_ge(stored[0], 16 * (NCH // 2))
            sp.wait_ge(stored[1], 16 * (NCH // 2))

        @block.tensor
        def _(pe):
            def up(c, e, k, first):
                u = 2 * e + k
                if u >= 3 or not first:
                    pe.wait_ge(hid_done, c * UNITS + u - 2)
                for w, bank in ((0, GB[u % 3]), (1, UB[u % 3])):
                    wh = wuph[:, w, e, P * k:P * k + P]
                    wl = wupl[:, w, e, P * k:P * k + P]
                    nc.tensor.matmul(bank[:, :], wh, xTh[:, bass.ds(c * TOK, TOK)], start=True, stop=False)
                    nc.tensor.matmul(bank[:, :], wh, xTl[:, bass.ds(c * TOK, TOK)], start=False, stop=False)
                    last = nc.tensor.matmul(bank[:, :], wl, xTh[:, bass.ds(c * TOK, TOK)], start=False, stop=True)
                last.then_inc(up_ready, 1)

            def down(c, e, par, first):
                pe.wait_ge(hid_done, c * UNITS + 2 * e + 2)
                if e >= 2 or not first:
                    pe.wait_ge(acc_done, c * SUMS + (e - 1) * CH)
                elif e == 0:
                    pe.wait_ge(wdn_in, 32)
                else:
                    pe.wait_ge(logit_done, 1)
                for i in range(CH):
                    for k in range(2):
                        u = 2 * e + k
                        last = nc.tensor.matmul(DB[(e + par) % 2][:, P * i:P * i + P], hid[u % 6][:, P * i:P * i + P],
                                                wdn32[:, e, k, :], start=(k == 0), stop=(k == 1))
                last.then_inc(down_ready, 1)

            def router():
                for t in range(TILES):
                    o = DB[1][:, E * t:E * t + E]
                    xh, xl = xTh[:, P * t:P * t + P], xTl[:, P * t:P * t + P]
                    nc.tensor.matmul(o, xh, wrh[:, :], start=(t == 0), stop=False, skip_group_check=True)
                    nc.tensor.matmul(o, xh, wrl[:, :], start=False, stop=False, skip_group_check=True)
                    last = nc.tensor.matmul(o, xl, wrh[:, :], start=False, stop=True, skip_group_check=True)
                last.then_inc(logit_ready, 1)

            def chunk(c, par, first=False):
                for e in range(E1):
                    up(c, e, 0, first)
                    up(c, e, 1, first)
                    if e:
                        down(c, e - 1, par, first)
                down(c, E1 - 1, par, first)

            router()
            chunk(0, 0, first=True)
            chunk(1, 1)
            with pe.Fori(1, NCH // 2, 1) as i:
                chunk(i * 2, 0)
                chunk(i * 2 + 1, 1)

        @block.scalar
        def _(act):
            act.wait_ge(logit_done, 1)
            nc.scalar.activation(pr[:, :, :], logit[:, :, :], ACT.Sigmoid).then_inc(pr_done, 1)

            def chunk(c, first=False):
                for u in range(UNITS):
                    act.wait_ge(up_ready, c * UNITS + u + 1)
                    if u >= 3 or not first:
                        act.wait_ge(hid_done, c * UNITS + u - 2)
                    nc.scalar.activation(sg[u % 3][:, :], GB[u % 3][:, :], ACT.Silu).then_inc(silu_done, 1)

            chunk(0, first=True)
            with act.Fori(1, NCH, 1) as c:
                chunk(c)

        @block.vector
        def _(dve):
            def hidden(c, u, first):
                dve.wait_ge(silu_done, c * UNITS + u + 1)
                if u >= 6 or not first:
                    dve.wait_ge(down_ready, c * E1 + (u - 6) // 2 + 1)
                nc.vector.tensor_tensor(hid[u % 6][:, :], sg[u % 3][:, :], UB[u % 3][:, :], ALU.mult).then_inc(hid_done, 1)

            def add(c, e, par):
                dve.wait_ge(down_ready, c * E1 + e + 1)
                if e:
                    dve.wait_ge(acc_done, c * SUMS + e * CH)
                for i in range(CH):
                    nc.vector.scalar_tensor_tensor(out=acc[par][:, i, :], in0=DB[(e + par) % 2][:, P * i:P * i + P],
                                                   scalar=cwc[par][:, i, e:e + 1], in1=acc[par][:, i, :],
                                                   op0=ALU.mult, op1=ALU.add).then_inc(acc_done, 1)

            def begin(c, par):
                if not isinstance(c, int) or c >= 2:
                    dve.wait_ge(stored[par], (c - par) * 8)
                nc.vector.tensor_copy(acc[par][:, :, :], R[:, bass.ds(c * CH, CH), :]).then_inc(acc_in, 1)
                nc.vector.tensor_copy(cwc[par][:, :, :], cw[:, bass.ds(c * CH, CH), :]).then_inc(cwc_done, 1)
                dve.wait_ge(acc_in, c + 1)
                dve.wait_ge(cwc_done, c + 1)

            def finish(c, par):
                dve.wait_ge(acc_done, (c + 1) * SUMS)
                normalise_rows(nc, dve, ln_chain, c * LN_STEPS(CH), acc[par], CH, lnst, lnmv, lntmp)
                for i in range(CH):
                    nc.vector.tensor_scalar(acc[par][:, i, :], acc[par][:, i, :], lnmv[:, i, 0:1],
                                            lntmp[:, 1, i:i + 1], ALU.subtract, ALU.mult).then_inc(fin_done, 1)

            def chunk(c, par, first=False):
                for e in range(E1):
                    hidden(c, 2 * e, first)
                    hidden(c, 2 * e + 1, first)
                    if e == 0:
                        begin(c, par)
                    if e:
                        add(c, e - 1, par)
                    if e == 1 and not first:
                        finish(c - 1, 1 - par)
                add(c, E1 - 1, par)

            def rank_experts():
                dve.wait_ge(pr_done, 1)
                mine = pr[:, :, :].unsqueeze(3).broadcast_to([P, TILES, E, E])
                other = pr[:, :, :].unsqueeze(2).broadcast_to([P, TILES, E, E])
                nc.vector.tensor_tensor(gt[:, :, :, :], other, mine, ALU.is_gt).then_inc(rank_steps, 1)
                nc.vector.tensor_tensor(eq[:, :, :, :], other, mine, ALU.is_equal).then_inc(rank_steps, 1)
                dve.wait_ge(rank_steps, 3)
                nc.vector.tensor_tensor(eq[:, :, :, :], eq[:, :, :, :], tri[:, :, :].unsqueeze(1).broadcast_to([P, TILES, E, E]),
                                        ALU.mult).then_inc(rank_steps, 1)
                dve.wait_ge(rank_steps, 4)
                nc.vector.tensor_tensor(gt[:, :, :, :], gt[:, :, :, :], eq[:, :, :, :], ALU.add).then_inc(rank_steps, 1)
                dve.wait_ge(rank_steps, 5)
                nc.vector.tensor_reduce(rank[:, :, :], gt[:, :, :, :], AX.X, ALU.add).then_inc(rank_steps, 1)
                dve.wait_ge(rank_steps, 6)
                nc.vector.scalar_tensor_tensor(out=cw[:, :, 1:E1], in0=rank[:, :, :], scalar=1.5, in1=pr[:, :, :],
                                               op0=ALU.is_lt, op1=ALU.mult).then_inc(cw_done, 1)
                dve.wait_ge(cw_done, 1)

            nc.vector.memset(cw[:, :, 0:1], 1.0).then_inc(rank_steps, 1)
            dve.wait_ge(logit_ready, 1)
            nc.vector.tensor_tensor(logit[:, :, :], DB[1][:, 0:TILES * E].rearrange("p (t e) -> p t e", e=E),
                                    rb_bc[:, :].unsqueeze(1).broadcast_to([P, TILES, E]), ALU.add).then_inc(logit_done, 1)
            rank_experts()
            chunk(0, 0, first=True)
            chunk(1, 1)
            with dve.Fori(1, NCH // 2, 1) as i:
                chunk(i * 2, 0)
                chunk(i * 2 + 1, 1)
            finish(NCH - 1, 1)


def kernel(L0_attn_x, L0_attn_Wattn, L0_attn_battn, L0_attn_Wproj, L0_attn_bproj, L0_attn_embk,
           L0_attn_embv, L0_ffn_Wg_s, L0_ffn_Wu_s, L0_ffn_Wd_s, L0_ffn_Wg, L0_ffn_Wu, L0_ffn_Wd,
           L0_ffn_Wr, L0_ffn_rb):
    import ml_dtypes
    import numpy as np
    import concourse.bacc as bacc
    from concourse.bass_utils import run_bass_kernel_spmd

    f = lambda a: np.ascontiguousarray(np.asarray(a))
    x = f(L0_attn_x)
    B, T, C = x.shape
    E = L0_ffn_Wr.shape[0]
    bqkv = f(L0_attn_battn)
    last = L0_attn_embk.shape[0] - 1
    far = np.clip(T - 1 - np.arange(T + 15), 0, last)
    far_v = np.clip(T - 1 - np.arange(T + 127), 0, last)
    gates = np.concatenate([f(L0_ffn_Wg_s)[None], f(L0_ffn_Wg)], 0)
    ups = np.concatenate([f(L0_ffn_Wu_s)[None], f(L0_ffn_Wu)], 0)
    downs = np.concatenate([f(L0_ffn_Wd_s)[None], f(L0_ffn_Wd)], 0)
    wup = np.stack([gates, ups], 0).transpose(3, 0, 1, 2)
    wdn = downs.reshape(E + 1, C, -1, 128).transpose(3, 0, 2, 1)
    p = np.arange(128)
    m8 = (p[None, :] % 8 == (p[:, None] // 8) % 8).astype(np.float16)
    mh = (p[None, :] // 8 == p[:, None] // 8).astype(np.float16)
    sel8 = (p[:, None] == p[None, :] % 8).astype(ml_dtypes.bfloat16)
    u = np.arange(24) - 8
    causal = np.where((u[None, :] > p[:, None]) & (p[:, None] < 8), -1e30, 0.0).astype(ml_dtypes.bfloat16)
    tri = np.broadcast_to(np.tril(np.ones((E, E), np.float32), -1).reshape(1, -1), (128, E * E))
    arrays = {
        "x": x, "xT": f(x.reshape(B * T, C).T), "Wqkv": f(L0_attn_Wattn),
        "bq": f(bqkv[0:C].reshape(C, 1)), "bk": f(bqkv[C:2 * C].reshape(C, 1)), "bv": f(bqkv[2 * C:]),
        "Wp": f(L0_attn_Wproj), "bp": f(L0_attn_bproj),
        "ekrev": f(f(L0_attn_embk)[far].T), "evrev": f(f(L0_attn_embv)[far_v]),
        "Wup": f(wup), "Wdn": f(wdn), "WrT": f(f(L0_ffn_Wr).T), "rb": f(L0_ffn_rb),
        "ident": np.eye(128, dtype=np.float32), "m8": m8, "mh": mh, "sel8": f(sel8), "causal": causal, "tri": f(tri),
    }
    nc = bacc.Bacc("TRN2", target_bir_lowering=False, num_devices=1)
    args = [nc.dram_tensor(f"in_{k}", a.shape, mybir.dt.from_np(a.dtype), kind="ExternalInput").ap()
            for k, a in arrays.items()]
    out = nc.dram_tensor("out_0", x.shape, F32, kind="ExternalOutput").ap()
    attention_and_experts(nc, *args, out)
    r = run_bass_kernel_spmd(nc, [{f"in_{k}": a for k, a in arrays.items()}], core_ids=[0])
    return r.results[0]["out_0"]
```

```python
from contextlib import ExitStack

import concourse.bass as bass
from concourse import mybir

ALU = mybir.AluOpType
ACT = mybir.ActivationFunctionType
AX = mybir.AxisListType
F32 = mybir.dt.float32
F16 = mybir.dt.float16
BF16 = mybir.dt.bfloat16

P = 128
EPS = 1e-5


def attention_and_experts(nc, x, xT, Wqkv, bqk, bv, Wp, bp, ekrows, evrows, Wup, Wdn, WrT, rb,
                          ident_in, m8_in, mh_in, sel8_in, causal_in, tri_in, out):
    B, T, C = x.shape
    H = 16
    D = C // H
    REL = T - P
    G = T // 8
    PAIRS = G // 2
    SCALE = 1.0 / float(D) ** 0.5
    E1 = Wup.shape[2]
    E = E1 - 1
    I = Wup.shape[3]
    TILES = B * T // P
    assert C == P and T == 2 * P and D == 8 and I == 2 * P and REL == P

    outer = ExitStack()
    with outer:
        def sem(name):
            return outer.enter_context(nc.semaphore(name))

        def keep(name, shape, dt):
            return outer.enter_context(nc.sbuf_tensor(name, shape, dt))

        R = keep("R", [P, TILES, C], F32)
        xTh = keep("xTh", [P, TILES * P], F16)
        xTl = keep("xTl", [P, TILES * P], F16)
        wuph = keep("wuph", [P, 2, E1, I], F16)
        wupl = keep("wupl", [P, 2, E1, I], F16)
        wrh = keep("wrh", [P, E], F16)
        wrl = keep("wrl", [P, E], F16)
        rb_bc = keep("rb_bc", [P, E], F32)
        ident = keep("ident", [P, P], F32)
        tri = keep("tri", [P, E, E], F32)
        z2 = keep("z2", [P, H, 8, 16], F32)
        yT1 = keep("yT1", [P, T], F32)
        yT2 = keep("yT2", [P, T], F32)
        den = keep("den", [P, T], F32)
        ysum = keep("ysum", [P, T], F32)
        rden = keep("rden", [P, T], F32)
        yT = keep("yT", [P, T], F32)
        xpb = keep("xpb", [P, 2, C], F32)
        rt = keep("rt", [P, 2, C], F32)
        lnst = keep("lnst", [P, 2, 6], F32)
        lnmv = keep("lnmv", [P, 2, 2], F32)
        lntmp = keep("lntmp", [P, 4, 2], F32)
        wp = keep("wp", [P, C], F32)
        y1d = [nc.dram_tensor(f"y1d{i}", [H, 2 * D, T], F32, kind="Internal").ap() for i in range(2)]
        y2d = [nc.dram_tensor(f"y2d{i}", [H, D, T], F32, kind="Internal").ap() for i in range(2)]

        y_spill = sem("y_spill")
        moe_weights_in = sem("moe_weights_in")
        w_split = sem("w_split")
        const_in = sem("const_in")

        att = ExitStack()
        with att:
            def sb(name, shape, dt):
                return att.enter_context(nc.sbuf_tensor(name, shape, dt))

            wup32 = R[:, TILES - E1 * I // C:TILES, :].rearrange("p (e k) c -> p e (k c)", e=E1)
            wr32 = sb("wr32", [P, E], F32)
            wqkv = sb("wqkv", [P, 3 * C], F32)
            bqk_col = sb("bqk_col", [P, 2], F32)
            bks_col = sb("bks_col", [P, 1], F32)
            bv_bc = sb("bv_bc", [P, C], F32)
            bp_bc = sb("bp_bc", [P, C], F32)
            m8 = sb("m8", [P, P], F16)
            mh = sb("mh", [P, P], F16)
            sel8 = sb("sel8", [P, P], BF16)
            causal = sb("causal", [P, 24], BF16)
            ESW = T + 8
            ek32 = sb("ek32", [P, ESW], F32)
            ekh = sb("ekh", [P, ESW], F16)
            ekl = sb("ekl", [P, ESW], F16)
            evw = sb("evw", [P, 2, 16, 8, D], F32)
            xTb = [sb(f"xTb{i}", [P, T], F32) for i in range(2)]
            xb = sb("xb", [P, 2, C], F32)
            qs = sb("qs", [P, 2, T], F16)
            qbd = [sb(f"qbd{i}", [P, 2, G, P], F16) for i in range(2)]
            q2rep = sb("q2rep", [P, H, T], F16)
            q2 = [sb(f"q2_{i}", [P, G, P], F16) for i in range(2)]
            kf = sb("kf", [P, T], F32)
            khi = [sb(f"khi{i}", [P, T], F16) for i in range(2)]
            klo = [sb(f"klo{i}", [P, T], F16) for i in range(2)]
            v1 = [sb(f"v1_{i}", [P, 2, H, 32], F32) for i in range(2)]
            nmax = sb("nmax", [P, G], F32)
            WB = [P * (g // (G // 2) + 1) for g in range(G)]
            PB = [sum(WB[:g]) for g in range(G)]
            prob = sb("prob", [P, sum(WB)], F32)
            pt0 = sb("pt0", [P, G * P], F32)
            pt1 = sb("pt1", [P, G * P // 2], F32)
            z1 = sb("z1", [P, H // 4, T], F32)

            S = [att.enter_context(nc.psum_tensor(f"S{i}", [P, 512], F32)) for i in range(4)]
            TB = [att.enter_context(nc.psum_tensor(f"TB{i}", [P, 512], F32)) for i in range(3)]
            XB = att.enter_context(nc.psum_tensor("XB", [P, 512], F32))

            qd = [nc.dram_tensor(f"qd{i}", [2, D, H, T], F16, kind="Internal").ap() for i in range(2)]

            early_in = sem("early_in")
            late_in = sem("late_in")
            zeroed = sem("zeroed")
            ek_ready = sem("ek_ready")
            bks_ready = sem("bks_ready")
            xT_in = [sem("xT_in0"), sem("xT_in1")]
            xb_in = sem("xb_in")
            qk_ready = sem("qk_ready")
            hi_done = sem("hi_done")
            qlo_done = sem("qlo_done")
            kf_done = sem("kf_done")
            klo_done = sem("klo_done")
            v_ready = sem("v_ready")
            v_done = sem("v_done")
            qbd_done = sem("qbd_done")
            q_spill = sem("q_spill")
            q2rep_in = sem("q2rep_in")
            q2_done = sem("q2_done")
            score_ready = sem("score_ready")
            max_done = sem("max_done")
            exp_done = sem("exp_done")
            tr_ready = sem("tr_ready")
            tr_out_a = sem("tr_out_a")
            tr_out_v = sem("tr_out_v")
            y_ready = sem("y_ready")
            y_out_a = sem("y_out_a")
            y_out_v = sem("y_out_v")
            y_back = sem("y_back")
            ysum_done = sem("ysum_done")
            rden_done = sem("rden_done")
            qbdl_done = sem("qbdl_done")
            st_done = sem("st_done")
            ln_chain = sem("ln_chain")
            x1_done = sem("x1_done")
            xturn_ready = sem("xturn_ready")
            xh_done = sem("xh_done")
            xl_done = sem("xl_done")
            wup_in = sem("wup_in")
            yT_done = sem("yT_done")
            xpb_done = sem("xpb_done")
            proj_ready = sem("proj_ready")
            r_done = sem("r_done")

            ORDER = [15, 14, 13, 12, 11, 10, 1, 0, 9, 8, 3, 2, 7, 6, 5, 4]
            assert sorted(ORDER) == list(range(PAIRS))

            def bank(o, par):
                return S[(o + 2 * par) % 4]

            GROUPS = [(28, 1), (28, 0), (24, 1), (24, 0), (20, 1), (20, 0), (0, 0), (16, 1), (16, 0), (4, 0), (12, 0),
                      (8, 0)]
            SLOT = [3, 4, 5, 6, 7, 8, 9, 11, 12, 13, None, None]
            NG = len(GROUPS)
            PT1_LAST = 7
            BY_ACT = [1, 3, 5, 6, 8, 10, 11]
            BY_DVE = [k for k in range(NG) if k not in BY_ACT]
            Y_ACT = [0, 2, 4]
            Y_DVE = [1, 3, 5]
            PIECES = 4
            HI_SLOT = [5, 8, 10, 11]
            Q2_SLOT = [12, 14, 15, 15]
            GP = G // PIECES
            Y_SPILLS = 4 + 16

            def count(k, ks):
                return sum(1 for j in ks if j <= k)

            def y_out_wait(eng, n, k):
                if k in Y_ACT:
                    eng.wait_ge(y_out_a, n * len(Y_ACT) + count(k, Y_ACT))
                else:
                    eng.wait_ge(y_out_v, n * len(Y_DVE) + count(k, Y_DVE))

            def group_out_wait(eng, n, k):
                if k in BY_ACT:
                    eng.wait_ge(tr_out_a, n * len(BY_ACT) + count(k, BY_ACT))
                else:
                    eng.wait_ge(tr_out_v, n * len(BY_DVE) + count(k, BY_DVE))

            block = att.enter_context(nc.Block())

            @block.sync
            def _(sp):
                def load_xT(m, par):
                    sp.dma_start(xTb[par][:, :], xT[:, bass.ds(m * T, T)]).then_inc(xT_in[par], 16)

                def load_xb(n):
                    sp.dma_start(xb[:, :, :], x[bass.ds(n, 1), :, :].rearrange(
                        "o (i p) c -> p (o i) c", p=P)).then_inc(xb_in, 16)

                def spill_q(m, par):
                    sp.wait_ge(qlo_done, m + 1)
                    for a in range(2):
                        sp.dma_start(qd[par][a].rearrange("d h t -> h d t"), qs[:, a, :]).then_inc(q_spill, 16)

                def spread_q(m, par):
                    sp.wait_ge(q_spill, m * 32 + 32)
                    if not (isinstance(m, int) and m == 0):
                        sp.wait_ge(q2_done, m)
                    for a in range(2):
                        src = qd[par][a].rearrange("d h t -> d (h t)")
                        sp.dma_start(q2rep[64 * a:64 * a + 64, :, :].rearrange("p h t -> p (h t)"),
                                     src.unsqueeze(0).broadcast_to([8, D, H * T])).then_inc(q2rep_in, 16)

                def spill_y1(n, par):
                    y_out_wait(sp, n, 0)
                    y_out_wait(sp, n, 1)
                    for hq in range(4):
                        sp.dma_start(y1d[par].rearrange("(j q) r t -> q r j t", q=4)[hq],
                                     z1[32 * hq:32 * hq + 2 * D, :, :]).then_inc(y_spill, 16)

                def spill_y2(n, par, half, rs):
                    if half == 0:
                        y_out_wait(sp, n, Y_ACT[-1])
                        y_out_wait(sp, n, Y_DVE[-1])
                    for r in rs:
                        row, tt = 64 * half + D * r, 7 - r
                        at = P * half + 16 * tt
                        sp.dma_start(y2d[par].rearrange("h d t -> d h t")[:, :, at:at + 16],
                                     z2[row:row + D, :, tt, :]).then_inc(y_spill, 16)

                def back_y(n, par):
                    sp.wait_ge(y_spill, (n + 1) * (16 * Y_SPILLS))
                    sp.wait_ge(yT_done, n + 1)
                    for dst, src in ((yT1, y1d[par][:, 0:D, :]), (den, y1d[par][:, D:2 * D, :]), (yT2, y2d[par])):
                        sp.dma_start(dst[:, :], src).then_inc(y_back, 16)

                def step(n, par, first=False, last=False):
                    if not last:
                        if not first:
                            sp.wait_ge(v_ready, n)
                        load_xT(n + 1, 1 - par)
                    if not first:
                        spill_y2(n - 1, 1 - par, 0, range(8))
                    if not last:
                        spill_q(n + 1, 1 - par)
                    if not first:
                        spill_y2(n - 1, 1 - par, 1, range(4))
                    if not last:
                        spread_q(n + 1, 1 - par)
                    if not first:
                        spill_y2(n - 1, 1 - par, 1, range(4, 8))
                        back_y(n - 1, 1 - par)
                        sp.wait_ge(xpb_done, n)
                    load_xb(n)
                    spill_y1(n, par)

                load_xT(0, 0)
                sp.dma_start(wqkv[:, :], Wqkv).then_inc(early_in, 16)
                sp.dma_start(bqk_col[:, :], bqk).then_inc(early_in, 16)
                sp.dma_start(bv_bc[:, :], bv.partition_broadcast(P)).then_inc(early_in, 16)
                for dst, src in ((mh, mh_in), (m8, m8_in), (ek32, ekrows), (sel8, sel8_in), (causal, causal_in),
                                 (ident, ident_in)):
                    sp.dma_start(dst[:, :], src).then_inc(const_in, 16)
                spill_q(0, 0)
                spread_q(0, 0)
                step(0, 0, first=True)
                with sp.Fori(0, B // 2 - 1, 1) as i:
                    step(i * 2 + 1, 1)
                    step(i * 2 + 2, 0)
                step(B - 1, 1, last=True)

            @block.gpsimd
            def _(pool):
                nc.gpsimd.memset(prob[:, :], 0.0).then_inc(zeroed, 1)
                pool.dma_start(bp_bc[:, :], bp.partition_broadcast(P)).then_inc(late_in, 16)
                pool.wait_ge(q2rep_in, 32)
                pool.dma_start(evw[:, :, :, :, :].rearrange("p b j r d -> p (b j r d)"), evrows).then_inc(late_in, 16)
                pool.dma_start(wp[:, :], Wp).then_inc(late_in, 16)
                pool.dma_start(wup32, Wup[:, 0, :, :]).then_inc(wup_in, 16)
                pool.dma_start(wr32[:, :], WrT).then_inc(moe_weights_in, 16)
                pool.dma_start(rb_bc[:, :], rb.partition_broadcast(P)).then_inc(moe_weights_in, 16)
                pool.dma_start(tri[:, :, :].rearrange("p a b -> p (a b)"), tri_in).then_inc(moe_weights_in, 16)
                pool.wait_ge(const_in, CONSTS)
                pool.wait_ge(late_in, LATE)

                def mask_q_lo(m, par):
                    pool.wait_ge(qlo_done, m + 1)
                    nc.gpsimd.tensor_tensor(qbd[par][:, 1, :, :].rearrange("p g (h t) -> p g h t", h=H),
                                            qs[:, 1, :].rearrange("p (g t) -> p g t", t=8).unsqueeze(2)
                                            .broadcast_to([P, G, H, 8]),
                                            mh[:, :].rearrange("p (h t) -> p h t", h=H).unsqueeze(1)
                                            .broadcast_to([P, G, H, 8]), ALU.mult).then_inc(qbdl_done, 1)

                def residual(n):
                    pool.wait_ge(xb_in, n * 16 + 16)
                    pool.wait_ge(r_done, n + 1)
                    nc.gpsimd.tensor_tensor(xpb[:, :, :], xb[:, :, :], bp_bc[:, :].unsqueeze(1).broadcast_to([P, 2, C]),
                                            ALU.add).then_inc(xpb_done, 1)

                mask_q_lo(1, 1)
                residual(0)
                for w in range(2):
                    pool.wait_ge(wup_in, 16 * (w + 1))
                    nc.gpsimd.tensor_copy(wuph[:, w, :, :], wup32).then_inc(w_split, 1)
                    pool.wait_ge(w_split, 2 * w + 1)
                    nc.gpsimd.tensor_tensor(wupl[:, w, :, :], wup32, wuph[:, w, :, :], ALU.subtract).then_inc(w_split, 1)
                    if w == 0:
                        pool.wait_ge(w_split, 2)
                        pool.dma_start(wup32, Wup[:, 1, :, :]).then_inc(wup_in, 16)
                        mask_q_lo(2, 0)
                residual(1)
                pool.wait_ge(moe_weights_in, 16 * 3)
                nc.gpsimd.tensor_copy(wrh[:, :], wr32[:, :]).then_inc(w_split, 1)
                pool.wait_ge(w_split, 5)
                nc.gpsimd.tensor_tensor(wrl[:, :], wr32[:, :], wrh[:, :], ALU.subtract).then_inc(w_split, 1)
                with pool.Fori(0, B // 2 - 2, 1) as i:
                    mask_q_lo(i * 2 + 3, 1)
                    residual(i * 2 + 2)
                    mask_q_lo(i * 2 + 4, 0)
                    residual(i * 2 + 3)
                mask_q_lo(B - 1, 1)
                residual(B - 2)
                residual(B - 1)

            @block.tensor
            def _(pe):
                def project_qk(m, par, halfm):
                    pe.wait_ge(xT_in[par], halfm * 16 + 16)
                    if not (isinstance(m, int) and m < 2):
                        pe.wait_ge(xl_done, m - 1)
                    nc.tensor.matmul(XB[:, 0:T], wqkv[:, 0:C], xTb[par][:, :], start=True, stop=True)
                    nc.tensor.matmul(XB[:, T:2 * T], wqkv[:, C:2 * C], xTb[par][:, :], start=True,
                                     stop=True).then_inc(qk_ready, 1)

                def project_v(m, par):
                    pe.wait_ge(kf_done, m + 1)
                    nc.tensor.matmul(XB[:, 0:C], xTb[par][:, 0:P], wqkv[:, 2 * C:3 * C], start=True, stop=True)
                    nc.tensor.matmul(XB[:, C:2 * C], xTb[par][:, P:T], wqkv[:, 2 * C:3 * C], start=True,
                                     stop=True).then_inc(v_ready, 1)

                def project_out(n, m):
                    pe.wait_ge(yT_done, n + 2)
                    pe.wait_ge(v_done, m)
                    pe.wait_ge(xl_done, n + 1)
                    nc.tensor.matmul(XB[:, 0:C], yT[:, 0:P], wp[:, :], start=True, stop=True)
                    nc.tensor.matmul(XB[:, C:2 * C], yT[:, P:T], wp[:, :], start=True,
                                     stop=True).then_inc(proj_ready, 1)

                def turn_rows(n):
                    pe.wait_ge(x1_done, n + 1)
                    for i in range(2):
                        last = nc.tensor.transpose(XB[:, P * i:P * i + P], rt[:, i, :], ident[:, :])
                    last.then_inc(xturn_ready, 1)

                def scores(n, par, o, first):
                    j = ORDER[o]
                    if o >= 4:
                        pe.wait_ge(exp_done, n * PAIRS + o - 3)
                    elif not first:
                        y_out_wait(pe, n - 1, o + 2)
                    W2 = 16 * (j + 1)
                    for a in range(2):
                        g = 2 * j + a
                        out_ = bank(o, par)[:, 256 * a:256 * a + W2]
                        qh = qbd[par][:, 0, g, :]
                        ql = qbd[par][:, 1, g, :]
                        qr = q2[par][:, g, :]
                        off = T - 8 - 8 * g
                        nc.tensor.matmul(out_, qh, khi[par][:, 0:W2], start=(a == 0), stop=False, skip_group_check=True)
                        nc.tensor.matmul(out_, qh, klo[par][:, 0:W2], start=False, stop=False, skip_group_check=True)
                        nc.tensor.matmul(out_, ql, khi[par][:, 0:W2], start=False, stop=False, skip_group_check=True)
                        nc.tensor.matmul(out_, qr, ekh[:, off:off + W2], start=False, stop=False, skip_group_check=True)
                        nc.tensor.matmul(out_, qr, ekl[:, off:off + W2], start=False, stop=False, skip_group_check=True)
                        last = nc.tensor.matmul(out_[:, W2 - 16:W2], sel8[:, :], causal[:, 8 - 8 * a:24 - 8 * a],
                                                start=False, stop=True, skip_group_check=True)
                    last.then_inc(score_ready, 1)

                def turn(n, k):
                    g0, blk = GROUPS[k]
                    done = 1 + max(ORDER.index(g0 // 2), ORDER.index(g0 // 2 + 1))
                    pe.wait_ge(exp_done, n * PAIRS + done)
                    if k >= 3:
                        group_out_wait(pe, n, k - 3)
                    for i in range(4):
                        at = PB[g0 + i] + P * blk
                        last = nc.tensor.transpose(TB[k % 3][:, P * i:P * i + P], prob[:, at:at + P],
                                                   ident[:, :])
                    last.then_inc(tr_ready, 1)

                def content(n, par, k, blk):
                    if blk == 1:
                        group_out_wait(pe, n, PT1_LAST)
                        pe.wait_ge(exp_done, n * PAIRS + 13 + k)
                    if blk == 0:
                        group_out_wait(pe, n, BY_ACT[-1])
                        group_out_wait(pe, n, BY_DVE[-1])
                    src = (pt1 if blk else pt0)[:, :].rearrange("p (g h t) -> p g h t", h=H, t=8)
                    for jj in range(2):
                        for hq in range(4):
                            h = 4 * (2 * k + jj) + hq
                            o = bank(k, par)[32 * hq:32 * hq + 32, T * jj + P * blk:T * jj + T]
                            last = nc.tensor.matmul(o, v1[par][:, blk, h, :], src[:, :, h, :],
                                                    start=(jj == 0 and blk == 1), stop=(blk == 0),
                                                    skip_group_check=True, tile_position=(0, 32 * hq))
                    if blk == 0:
                        last.then_inc(y_ready, 1)

                def relative(n, par, loads):
                    if isinstance(n, int) and n == 0:
                        pe.wait_ge(late_in, LATE)
                    p0 = pt0[:, :].rearrange("p (b tt a h t) -> p b tt a h t", b=2, a=2, h=H, t=8)
                    p1 = pt1[:, :].rearrange("p (tt a h t) -> p tt a h t", a=2, h=H, t=8)
                    for k in loads:
                        if k >= 4:
                            y_out_wait(pe, n, k - 4)
                        for jj in range(4):
                            j = 4 * (k - 2) + jj
                            for half, blk in ((0, 0), (1, 0), (1, 1)):
                                lhs = evw[:, 1 - (half - blk), 15 - j, :, :].rearrange("p r d -> p (r d)")
                                src = p1[:, :, j // 8, :, j % 8] if blk else p0[:, half, :, j // 8, :, j % 8]
                                last = nc.tensor.matmul(bank(k, par)[64 * half:64 * half + 64, P * jj:P * jj + P], lhs, src,
                                                        start=(jj == 0 and blk == 0), stop=(half == blk),
                                                        skip_group_check=True, tile_position=(0, 64 * half))
                        last.then_inc(y_ready, 1)

                def step(n, par, halfm, first=False, last=False):
                    pe.wait_ge(qbd_done, n + 1)
                    pe.wait_ge(qbdl_done, n + 1)
                    pe.wait_ge(klo_done, n + 1)
                    pe.wait_ge(q2_done, n + 1)
                    pe.wait_ge(v_done, n + 1)
                    for o in range(PAIRS):
                        scores(n, par, o, first)
                        if o == 2 and not last:
                            project_qk(n + 1, 1 - par, halfm)
                        for k in range(NG):
                            if SLOT[k] == o:
                                turn(n, k)
                    content(n, par, 0, 1)
                    turn(n, NG - 2)
                    content(n, par, 1, 1)
                    turn(n, NG - 1)
                    if not last:
                        project_v(n + 1, 1 - par)
                    content(n, par, 0, 0)
                    content(n, par, 1, 0)
                    if not first:
                        project_out(n - 1, n + 1 if last else n + 2)
                    relative(n, par, range(2, 6))
                    if not first:
                        turn_rows(n - 1)

                pe.wait_ge(early_in, 48)
                project_qk(0, 0, 0)
                project_v(0, 0)
                pe.wait_ge(const_in, CONSTS)
                pe.wait_ge(ek_ready, 2)
                pe.wait_ge(zeroed, ZEROS)
                step(0, 0, 0, first=True)
                with pe.Fori(0, B // 2 - 1, 1) as i:
                    step(i * 2 + 1, 1, i + 1)
                    step(i * 2 + 2, 0, i + 1)
                step(B - 1, 1, 0, last=True)

            @block.scalar
            def _(act):
                def split_hi(m, par):
                    act.wait_ge(qk_ready, m + 1)
                    if not (isinstance(m, int) and m == 0):
                        act.wait_ge(qbd_done, m)
                        act.wait_ge(q_spill, m * 32)
                    nc.scalar.activation(qs[:, 0, :], XB[:, 0:T], ACT.Identity, bias=bqk_col[:, 0:1])
                    nc.scalar.activation(khi[par][:, :], XB[:, T:2 * T], ACT.Identity, bias=bks_col[:, 0:1],
                                         scale=SCALE).then_inc(hi_done, 1)

                def exps(n, par, o):
                    j = ORDER[o]
                    act.wait_ge(max_done, n * PAIRS + o + 1)
                    W2 = 16 * (j + 1)
                    for a in range(2):
                        g = 2 * j + a
                        last = nc.scalar.activation(prob[:, PB[g]:PB[g] + W2], bank(o, par)[:, 256 * a:256 * a + W2],
                                                    ACT.Exp, bias=nmax[:, g:g + 1])
                    last.then_inc(exp_done, 1)

                def turned(n, k):
                    g0, blk = GROUPS[k]
                    act.wait_ge(tr_ready, n * NG + k + 1)
                    dst = pt1[:, P * (g0 - G // 2):P * (g0 - G // 2) + 512] if blk else pt0[:, P * g0:P * g0 + 512]
                    nc.scalar.activation(dst, TB[k % 3][:, :], ACT.Copy).then_inc(tr_out_a, 1)

                def step(n, par, first=False, last=False):
                    for o in range(PAIRS):
                        exps(n, par, o)
                        if o == 2 and not last:
                            split_hi(n + 1, 1 - par)
                        for k in BY_ACT:
                            if SLOT[k] == o:
                                turned(n, k)
                    turned(n, NG - 2)
                    turned(n, NG - 1)
                    if not first:
                        act.wait_ge(y_spill, n * (16 * Y_SPILLS))
                    for k in Y_ACT:
                        act.wait_ge(y_ready, n * 6 + k + 1)
                        if k == 0:
                            nc.scalar.activation(z1[:, 0:2, :], bank(0, par)[:, :], ACT.Copy).then_inc(y_out_a, 1)
                        else:
                            j0 = 4 * (k - 2)
                            nc.scalar.activation(z2[:, :, :, j0:j0 + 4].rearrange("p h t j -> p j t h"),
                                                 bank(k, par)[:, :].rearrange("p (j t h) -> p j t h", j=4, t=8),
                                                 ACT.Copy).then_inc(y_out_a, 1)
                    if not first:
                        rows_hi(n - 1)

                def rows_hi(n):
                    act.wait_ge(xturn_ready, n + 1)
                    nc.scalar.activation(xTh[:, bass.ds(n * T, T)], XB[:, 0:T], ACT.Copy).then_inc(xh_done, 1)

                act.wait_ge(early_in, 48)
                act.wait_ge(bks_ready, 1)
                split_hi(0, 0)
                act.wait_ge(zeroed, ZEROS)
                step(0, 0, first=True)
                with act.Fori(0, B // 2 - 1, 1) as i:
                    step(i * 2 + 1, 1)
                    step(i * 2 + 2, 0)
                step(B - 1, 1, last=True)

            @block.vector
            def _(dve):
                def split_lo(m, par):
                    dve.wait_ge(hi_done, m + 1)
                    if not (isinstance(m, int) and m == 0):
                        dve.wait_ge(qbdl_done, m)
                    nc.vector.scalar_tensor_tensor(out=qs[:, 1, :], in0=XB[:, 0:T], scalar=bqk_col[:, 0:1],
                                                   in1=qs[:, 0, :], op0=ALU.add, op1=ALU.subtract).then_inc(qlo_done, 1)
                    if not (isinstance(m, int) and m == 0):
                        dve.wait_ge(klo_done, m)
                    nc.vector.tensor_scalar(kf[:, :], XB[:, T:2 * T], bqk_col[:, 1:2], SCALE, ALU.add,
                                            ALU.mult).then_inc(kf_done, 1)
                    dve.wait_ge(kf_done, m + 1)
                    nc.vector.tensor_tensor(klo[par][:, :], kf[:, :], khi[par][:, :],
                                            ALU.subtract).then_inc(klo_done, 1)

                def take_v(m, par):
                    dve.wait_ge(v_ready, m + 1)
                    nc.vector.tensor_tensor(v1[par][:, :, :, 0:D],
                                            XB[:, 0:2 * C].rearrange("p (b h d) -> p b h d", b=2, h=H),
                                            bv_bc[:, :].rearrange("p (h d) -> p h d", h=H).unsqueeze(1)
                                            .broadcast_to([P, 2, H, D]), ALU.add).then_inc(v_done, 1)

                def mask_q2(m, par, p):
                    dve.wait_ge(q2rep_in, (m + 1) * 32)
                    ins = nc.vector.tensor_tensor(q2[par][:, p * GP:p * GP + GP, :].rearrange("p g (h t) -> p g h t", h=H),
                                            q2rep[:, :, 8 * p * GP:8 * (p + 1) * GP].rearrange("p h (g t) -> p g h t", t=8),
                                            m8[:, :].rearrange("p (h t) -> p h t", h=H).unsqueeze(1)
                                            .broadcast_to([P, GP, H, 8]), ALU.mult)
                    if p == PIECES - 1:
                        ins.then_inc(q2_done, 1)

                def mask_q(m, par, p):
                    ins = nc.vector.tensor_tensor(qbd[par][:, 0, p * GP:p * GP + GP, :].rearrange("p g (h t) -> p g h t", h=H),
                                            qs[:, 0, 8 * p * GP:8 * (p + 1) * GP].rearrange("p (g t) -> p g t", t=8)
                                            .unsqueeze(2).broadcast_to([P, GP, H, 8]),
                                            mh[:, :].rearrange("p (h t) -> p h t", h=H).unsqueeze(1)
                                            .broadcast_to([P, GP, H, 8]), ALU.mult)
                    if p == PIECES - 1:
                        ins.then_inc(qbd_done, 1)

                def maxima(n, par, o):
                    j = ORDER[o]
                    W2 = 16 * (j + 1)
                    dve.wait_ge(score_ready, n * PAIRS + o + 1)
                    nc.vector.tensor_reduce(nmax[:, 2 * j:2 * j + 2],
                                            bank(o, par)[:, :].rearrange("p (a w) -> p a w", a=2)[:, :, 0:W2],
                                            AX.X, ALU.max, negate=True).then_inc(max_done, 1)

                def turned(n, k):
                    g0, blk = GROUPS[k]
                    dve.wait_ge(tr_ready, n * NG + k + 1)
                    dst = pt1[:, P * (g0 - G // 2):P * (g0 - G // 2) + 512] if blk else pt0[:, P * g0:P * g0 + 512]
                    nc.vector.tensor_copy(dst, TB[k % 3][:, :]).then_inc(tr_out_v, 1)

                def invert(n, half):
                    dve.wait_ge(y_back, n * 48 + 48)
                    nc.vector.reciprocal(rden[:, P * half:P * half + P], den[:, P * half:P * half + P]).then_inc(rden_done, 1)

                def normalise(n):
                    nc.vector.tensor_tensor(ysum[:, :], yT1[:, :], yT2[:, :], ALU.add).then_inc(ysum_done, 1)
                    dve.wait_ge(ysum_done, n + 1)
                    dve.wait_ge(rden_done, n * 2 + 2)
                    nc.vector.tensor_tensor(yT[:, :], ysum[:, :], rden[:, :], ALU.mult).then_inc(yT_done, 1)

                def residual(n):
                    dve.wait_ge(proj_ready, n + 1)
                    dve.wait_ge(xpb_done, n + 1)
                    nc.vector.tensor_tensor(rt[:, :, :], XB[:, 0:2 * C].rearrange("p (i c) -> p i c", i=2),
                                            xpb[:, :, :], ALU.add).then_inc(r_done, 1)

                def layer_norm(n):
                    dve.wait_ge(r_done, n + 2)
                    for stage in range(LN_STAGES):
                        normalise_rows(nc, dve, ln_chain, n * LN_STEPS(2), rt, 2, lnst, lnmv, lntmp, stage)
                    for i in range(2):
                        last = nc.vector.tensor_scalar(rt[:, i, :], rt[:, i, :], lnmv[:, i, 0:1], lntmp[:, 1, i:i + 1],
                                                       ALU.subtract, ALU.mult)
                    last.then_inc(x1_done, 1)

                def keep_rows(n):
                    dve.wait_ge(x1_done, n + 1)
                    dve.wait_ge(w_split, 4)
                    nc.vector.tensor_copy(R[:, bass.ds(n * 2, 2), :], rt[:, :, :]).then_inc(st_done, 1)

                def rows_lo(n):
                    dve.wait_ge(xh_done, n + 1)
                    nc.vector.tensor_tensor(xTl[:, bass.ds(n * T, T)], XB[:, 0:T], xTh[:, bass.ds(n * T, T)],
                                            ALU.subtract).then_inc(xl_done, 1)

                def take_y(n, par, k):
                    dve.wait_ge(y_ready, n * 6 + k + 1)
                    if k == 1:
                        nc.vector.tensor_copy(z1[:, 2:4, :], bank(1, par)[:, :].rearrange("p (j t) -> p j t", j=2)).then_inc(y_out_v, 1)
                    else:
                        j0 = 4 * (k - 2)
                        nc.vector.tensor_copy(z2[:, :, :, j0:j0 + 4].rearrange("p h t j -> p j t h"),
                                              bank(k, par)[:, :].rearrange("p (j t h) -> p j t h", j=4, t=8)).then_inc(y_out_v, 1)

                def step(n, par, first=False, last=False):
                    for o in range(PAIRS):
                        maxima(n, par, o)
                        if o == 3 and not last:
                            split_lo(n + 1, 1 - par)
                        for p in range(PIECES):
                            if HI_SLOT[p] == o and not last:
                                mask_q(n + 1, 1 - par, p)
                        for p in range(PIECES):
                            if Q2_SLOT[p] == o and not last:
                                mask_q2(n + 1, 1 - par, p)
                        for k in BY_DVE:
                            if SLOT[k] == o:
                                turned(n, k)
                    if not first:
                        invert(n - 1, 0)
                    if not last:
                        take_v(n + 1, 1 - par)
                    if not first:
                        invert(n - 1, 1)
                        normalise(n - 1)
                        dve.wait_ge(y_spill, n * (16 * Y_SPILLS))
                    take_y(n, par, 1)
                    if not first:
                        residual(n - 1)
                        layer_norm(n - 1)
                    take_y(n, par, 3)
                    take_y(n, par, 5)
                    if not first:
                        keep_rows(n - 1)
                        rows_lo(n - 1)

                for par in range(2):
                    nc.vector.memset(v1[par][:, :, :, D:32], 1.0).then_inc(zeroed, 1)
                nc.vector.memset(ysum[:, :], 0.0).then_inc(r_done, 1)
                nc.vector.memset(rden[:, :], 0.0).then_inc(xl_done, 1)
                nc.vector.memset(yT[:, :], 0.0).then_inc(yT_done, 1)
                nc.vector.memset(ekl[64:P, :], 0.0).then_inc(zeroed, 1)
                dve.wait_ge(early_in, 48)
                nc.vector.tensor_scalar(bks_col[:, :], bqk_col[:, 1:2], SCALE, None, ALU.mult).then_inc(bks_ready, 1)
                split_lo(0, 0)
                take_v(0, 0)
                dve.wait_ge(const_in, CONSTS)
                for p in range(PIECES):
                    mask_q(0, 0, p)
                nc.vector.tensor_tensor(qbd[0][:, 1, :, :].rearrange("p g (h t) -> p g h t", h=H),
                                        qs[:, 1, :].rearrange("p (g t) -> p g t", t=8).unsqueeze(2)
                                        .broadcast_to([P, G, H, 8]),
                                        mh[:, :].rearrange("p (h t) -> p h t", h=H).unsqueeze(1)
                                        .broadcast_to([P, G, H, 8]), ALU.mult).then_inc(qbdl_done, 1)
                nc.vector.tensor_copy(ekh[:, :], ek32[:, :]).then_inc(ek_ready, 1)
                dve.wait_ge(ek_ready, 1)
                nc.vector.tensor_tensor(ekl[0:64, :], ek32[0:64, :], ekh[0:64, :], ALU.subtract).then_inc(ek_ready, 1)
                for p in range(PIECES):
                    mask_q2(0, 0, p)
                step(0, 0, first=True)
                with dve.Fori(0, B // 2 - 1, 1) as i:
                    step(i * 2 + 1, 1)
                    step(i * 2 + 2, 0)
                step(B - 1, 1, last=True)

        last = LastSequence(T, y1d[1], y2d[1], y_spill, 16 * (Y_SPILLS * (B - 1) + 4))
        last.z2, last.yT1, last.yT2, last.den, last.ysum, last.rden, last.yT = z2, yT1, yT2, den, ysum, rden, yT
        last.wp, last.xpb, last.rt, last.ident = wp, xpb, rt, ident
        last.lnst, last.lnmv, last.lntmp = lnst, lnmv, lntmp
        experts(nc, sem, last, E, E1, I, TILES, R, xTh, xTl, wuph, wupl, Wdn, wrh, wrl, rb_bc, tri, out)


CONSTS = 16 * 6
LATE = 16 * 3
ZEROS = 1 + 3


LN_STAGES = 4


class LastSequence:

    def __init__(self, T, y1d, y2d, y_spill, y_spilled):
        self.T, self.y1d, self.y2d, self.y_spill, self.y_spilled = T, y1d, y2d, y_spill, y_spilled


def LN_STEPS(rows):
    return 2 * rows + 12


def normalise_rows(nc, dve, chain, base, src, rows, st, mv, tmp, stage):
    done = [0 if stage == 0 else 2 * rows + 3 * stage]

    def link(ins):
        done[0] += 1
        ins.then_inc(chain, 1)

    def linked(ins):
        link(ins)
        dve.wait_ge(chain, base + done[0])

    ve, r, t = tmp[:, 0, 0:rows], tmp[:, 1, 0:rows], tmp[:, 2, 0:rows]
    if stage == 0:
        for i in range(rows):
            link(nc.vector.bn_stats(st[:, i, :], src[:, i, :]))
        dve.wait_ge(chain, base + done[0])
        nc.vector.memset(tmp[:, 3, 0:1], 0.0)
        for i in range(rows):
            link(nc.vector.bn_aggr(mv[:, i, :], st[:, i, :]))
        dve.wait_ge(chain, base + done[0])
        I32 = mybir.dt.int32
        linked(nc.vector.tensor_scalar(ve, mv[:, :, 1], EPS, None, ALU.add))
        linked(nc.vector.tensor_scalar(t.bitcast(I32), ve.bitcast(I32), 1, None, ALU.logical_shift_right))
        linked(nc.vector.tensor_scalar(r.bitcast(I32), t.bitcast(I32), -1.0, float(0x5f3759df), ALU.mult, ALU.add))
        assert done[0] == 2 * rows + 3
    else:
        linked(nc.vector.scalar_tensor_tensor(out=t, in0=r, scalar=-0.5, in1=r, op0=ALU.mult, op1=ALU.mult))
        linked(nc.vector.tensor_tensor(t, t, ve, ALU.mult))
        linked(nc.vector.scalar_tensor_tensor(out=r, in0=t, scalar=1.5, in1=r, op0=ALU.add, op1=ALU.mult))


def experts(nc, sem, last, E, E1, I, TILES, R, xTh, xTl, wuph, wupl, Wdn, wrh, wrl, rb_bc, tri, out):
    C = P
    CH = 4
    NCH = TILES // CH
    TOK = CH * P
    T = last.T
    NL = TILES - T // P
    ctx = ExitStack()
    with ctx:
        def sb(name, shape, dt):
            return ctx.enter_context(nc.sbuf_tensor(name, shape, dt))

        def ps(name):
            return ctx.enter_context(nc.psum_tensor(name, [P, 512], F32))

        acc = [sb(f"acc{i}", [P, CH, C], F32) for i in range(2)]
        wdn32 = sb("wdn32", [P, E1, 2, C], F32)
        wdnh = sb("wdnh", [P, E1, 2, C], F16)
        wdnl = sb("wdnl", [P, E1, 2, C], F16)
        lnst = sb("lnst2", [P, CH, 6], F32)
        lnmv = sb("lnmv2", [P, CH, 2], F32)
        lntmp = sb("lntmp2", [P, 4, CH], F32)
        logit = sb("logit", [P, TILES, E], F32)
        pr = sb("pr", [P, TILES, E], F32)
        prc = sb("prc", [P, CH, E], F32)
        gt = sb("gt", [P, CH, E, E], F32)
        eq = sb("eq", [P, CH, E, E], F32)
        rank = sb("rank", [P, CH, E], F32)
        cwc = [sb(f"cwc{i}", [P, CH, E1], F32) for i in range(2)]
        sg = [sb(f"sg{i}", [P, TOK], F32) for i in range(3)]
        hid = [sb(f"hid{i}", [P, TOK], F32) for i in range(3)]
        hidh = [sb(f"hidh{i}", [P, TOK], F16) for i in range(6)]
        hidl = [sb(f"hidl{i}", [P, TOK], F16) for i in range(6)]

        GB = [ps(f"GB{i}") for i in range(2)]
        UB = [ps(f"UB{i}") for i in range(3)]
        DB = [ps(f"DB{i}") for i in range(2)]
        MX = ps("MX")
        LG = MX[:, T:T + TILES * E]

        wdn_in = [sem("wdn_in0"), sem("wdn_in1")]
        wdnh_done = sem("wdnh_done")
        wdnl_done = sem("wdnl_done")
        logit_ready = sem("logit_ready")
        logit_done = sem("logit_done")
        pr_done = sem("pr_done")
        rank_chain = sem("rank_chain")
        ones_done = sem("ones_done")
        acc_in = sem("acc_in")
        up_ready = sem("up_ready")
        silu_done = sem("silu_done")
        hid_done = sem("hid_done")
        hi_done = sem("hidh_done")
        lo_done = sem("hidl_done")
        down_ready = sem("down_ready")
        acc_done = sem("acc_done")
        ln_chain = sem("ln_chain2")
        fin_done = sem("fin_done")
        stored = [sem("stored0"), sem("stored1")]
        last_spill = sem("last_spill")
        last_back = sem("last_back")
        last_chain = sem("last_chain")
        last_y = sem("last_y")
        last_proj = sem("last_proj")
        last_r = sem("last_r")
        last_ln = sem("last_ln")
        last_x1 = sem("last_x1")
        last_turned = sem("last_turned")
        last_xh = sem("last_xh")
        last_xl = sem("last_xl")

        UNITS = 2 * E1
        SUMS = E1 * CH
        WPARTS = ((0, 2), (2, E1))
        assert E1 % 2 == 1 and UNITS % 6 == 0
        block = ctx.enter_context(nc.Block())

        @block.sync
        def _(sp):
            o = out.rearrange("b (i p) c -> p (b i) c", p=P)
            for part, (a, b) in enumerate(WPARTS):
                sp.dma_start(wdn32[:, a:b, :, :], Wdn[:, a:b, :, :]).then_inc(wdn_in[part], 16)
            D = last.y2d.shape[1]
            for half in range(2):
                for r in range(8):
                    row, tt = 64 * half + D * r, 7 - r
                    at = P * half + 16 * tt
                    sp.dma_start(last.y2d.rearrange("h d t -> d h t")[:, :, at:at + 16],
                                 last.z2[row:row + D, :, tt, :]).then_inc(last_spill, 16)
            sp.wait_ge(last.y_spill, last.y_spilled)
            sp.wait_ge(last_spill, 16 * 16)
            for dst, src in ((last.yT1, last.y1d[:, 0:D, :]), (last.den, last.y1d[:, D:2 * D, :]),
                             (last.yT2, last.y2d)):
                sp.dma_start(dst[:, :], src).then_inc(last_back, 16)
            with sp.Fori(0, NCH // 2, 1) as i:
                for par in range(2):
                    sp.wait_ge(fin_done, (i * 2 + par + 1) * CH)
                    sp.dma_start(o[:, bass.ds((i * 2 + par) * CH, CH), :], acc[par][:, :, :]).then_inc(stored[par], 16)
            sp.wait_ge(stored[0], 16 * (NCH // 2))
            sp.wait_ge(stored[1], 16 * (NCH // 2))

        @block.tensor
        def _(pe):
            def up(c, u, first):
                e, k = u // 2, u % 2
                if u >= 2 or not first:
                    pe.wait_ge(silu_done, c * UNITS + u - 1)
                if u >= 3 or not first:
                    pe.wait_ge(hid_done, c * UNITS + u - 2)
                for w, bank in ((0, GB[u % 2]), (1, UB[u % 3])):
                    wh = wuph[:, w, e, P * k:P * k + P]
                    wl = wupl[:, w, e, P * k:P * k + P]
                    nc.tensor.matmul(bank[:, :], wh, xTh[:, bass.ds(c * TOK, TOK)], start=True, stop=False)
                    nc.tensor.matmul(bank[:, :], wh, xTl[:, bass.ds(c * TOK, TOK)], start=False, stop=False)
                    end = nc.tensor.matmul(bank[:, :], wl, xTh[:, bass.ds(c * TOK, TOK)], start=False, stop=True)
                end.then_inc(up_ready, 1)

            def down(c, e, par, first=False):
                pe.wait_ge(hi_done, c * UNITS + 2 * e + 2)
                pe.wait_ge(lo_done, c * UNITS + 2 * e + 2)
                if e >= 2 or not first:
                    pe.wait_ge(acc_done, c * SUMS + (e - 1) * CH)
                if first and e == 0:
                    pe.wait_ge(wdnl_done, 1)
                if first and e == WPARTS[1][0]:
                    pe.wait_ge(wdnl_done, 2)
                ew = e % E1
                for i in range(CH):
                    for k in range(2):
                        hh, hl = (t[(2 * e + k) % 6][:, P * i:P * i + P] for t in (hidh, hidl))
                        o = DB[(e + par) % 2][:, P * i:P * i + P]
                        nc.tensor.matmul(o, hh, wdnh[:, ew, k, :], start=(k == 0), stop=False)
                        nc.tensor.matmul(o, hh, wdnl[:, ew, k, :], start=False, stop=False)
                        end = nc.tensor.matmul(o, hl, wdnh[:, ew, k, :], start=False, stop=(k == 1))
                end.then_inc(down_ready, 1)

            def router(t0, t1):
                for t in range(t0, t1):
                    o = LG[:, E * t:E * t + E]
                    xh, xl = xTh[:, P * t:P * t + P], xTl[:, P * t:P * t + P]
                    nc.tensor.matmul(o, xh, wrh[:, :], start=(t == t0), stop=False, skip_group_check=True)
                    nc.tensor.matmul(o, xh, wrl[:, :], start=False, stop=False, skip_group_check=True)
                    end = nc.tensor.matmul(o, xl, wrh[:, :], start=False, stop=True, skip_group_check=True)
                end.then_inc(logit_ready, 1)

            def chunk(c, par, first=False):
                for e in range(E1):
                    up(c, 2 * e, first)
                    if e >= 2 or not first:
                        down(c, e - 2, par, first)
                    up(c, 2 * e + 1, first)
                    if first and e == 4:
                        pe.wait_ge(last_y, 1)
                        pe.wait_ge(logit_done, 1)
                        nc.tensor.matmul(MX[:, 0:C], last.yT[:, 0:P], last.wp[:, :], start=True, stop=True)
                        nc.tensor.matmul(MX[:, C:2 * C], last.yT[:, P:T], last.wp[:, :], start=True,
                                         stop=True).then_inc(last_proj, 1)
                    if first and e == 7:
                        pe.wait_ge(last_x1, 2)
                        for i in range(2):
                            end = nc.tensor.transpose(MX[:, P * i:P * i + P], last.rt[:, i, :], last.ident[:, :])
                        end.then_inc(last_turned, 1)
                if first:
                    pe.wait_ge(last_xh, 1)
                    pe.wait_ge(last_xl, 1)
                    router(CH, TILES)

            router(0, CH)
            chunk(0, 0, first=True)
            chunk(1, 1)
            with pe.Fori(1, NCH // 2, 1) as i:
                chunk(i * 2, 0)
                chunk(i * 2 + 1, 1)
            down(NCH, -2, 0)
            down(NCH, -1, 0)

        @block.scalar
        def _(act):
            def weights_hi(part):
                a, b = WPARTS[part]
                act.wait_ge(wdn_in[part], 16)
                nc.scalar.activation(wdnh[:, a:b, :, :], wdn32[:, a:b, :, :], ACT.Copy).then_inc(wdnh_done, 1)

            def silu(c, u, first):
                act.wait_ge(up_ready, c * UNITS + u + 1)
                if u >= 3 or not first:
                    act.wait_ge(hid_done, c * UNITS + u - 2)
                nc.scalar.activation(sg[u % 3][:, :], GB[u % 2][:, :], ACT.Silu).then_inc(silu_done, 1)

            def hi(c, u, first):
                act.wait_ge(hid_done, c * UNITS + u + 1)
                if u >= 6 or not first:
                    act.wait_ge(down_ready, c * E1 + (u - 6) // 2 + 1)
                nc.scalar.activation(hidh[u % 6][:, :], hid[u % 3][:, :], ACT.Copy).then_inc(hi_done, 1)

            def chunk(c, first=False, second=False):
                for u in range(UNITS):
                    silu(c, u, first)
                    if u or not first:
                        hi(c, u - 1, first)
                    if first and u == 1:
                        weights_hi(0)
                    if first and u == 3:
                        weights_hi(1)
                    if first and u == 15:
                        act.wait_ge(last_turned, 1)
                        nc.scalar.activation(xTh[:, P * NL:P * NL + T], MX[:, 0:T], ACT.Copy).then_inc(last_xh, 1)
                    if second and u == 1:
                        act.wait_ge(logit_done, 2)
                        nc.scalar.activation(pr[:, CH:, :], logit[:, CH:, :], ACT.Sigmoid).then_inc(pr_done, 1)

            act.wait_ge(logit_done, 1)
            nc.scalar.activation(pr[:, 0:CH, :], logit[:, 0:CH, :], ACT.Sigmoid).then_inc(pr_done, 1)
            chunk(0, first=True)
            chunk(1, second=True)
            with act.Fori(2, NCH, 1) as c:
                chunk(c)
            hi(NCH, -1, False)

        @block.gpsimd
        def _(pool):
            def lo(c, u):
                pool.wait_ge(hi_done, c * UNITS + u + 1)
                nc.gpsimd.tensor_tensor(hidl[u % 6][:, :], hid[u % 3][:, :], hidh[u % 6][:, :],
                                        ALU.subtract).then_inc(lo_done, 1)

            with pool.Fori(0, NCH, 1) as c:
                for u in range(UNITS):
                    lo(c, u)

        @block.vector
        def _(dve):
            def weights_lo(part):
                a, b = WPARTS[part]
                dve.wait_ge(wdnh_done, part + 1)
                nc.vector.tensor_tensor(wdnl[:, a:b, :, :], wdn32[:, a:b, :, :], wdnh[:, a:b, :, :],
                                        ALU.subtract).then_inc(wdnl_done, 1)

            def hidden(c, u, first):
                dve.wait_ge(silu_done, c * UNITS + u + 1)
                if u >= 3 or not first:
                    dve.wait_ge(lo_done, c * UNITS + u - 2)
                nc.vector.tensor_tensor(hid[u % 3][:, :], sg[u % 3][:, :], UB[u % 3][:, :], ALU.mult).then_inc(hid_done, 1)

            def add(c, e, par):
                dve.wait_ge(down_ready, c * E1 + e + 1)
                if e != 0:
                    dve.wait_ge(acc_done, c * SUMS + e * CH)
                ew = e % E1
                bank = DB[(e + par) % 2] if e >= 0 else DB[(e + 1 - par) % 2]
                for i in range(CH):
                    nc.vector.scalar_tensor_tensor(out=acc[par][:, i, :], in0=bank[:, P * i:P * i + P],
                                                   scalar=cwc[par][:, i, ew:ew + 1], in1=acc[par][:, i, :],
                                                   op0=ALU.mult, op1=ALU.add).then_inc(acc_done, 1)

            def begin(c, par):
                if not isinstance(c, int) or c >= 2:
                    dve.wait_ge(stored[par], (c - par) * 8)
                nc.vector.tensor_copy(acc[par][:, :, :], R[:, bass.ds(c * CH, CH), :]).then_inc(acc_in, 1)

            def rank_experts(c, par):
                mine = prc[:, :, :].unsqueeze(3).broadcast_to([P, CH, E, E])
                other = prc[:, :, :].unsqueeze(2).broadcast_to([P, CH, E, E])
                dve.wait_ge(pr_done, 1 if isinstance(c, int) and c == 0 else 2)
                nc.vector.tensor_copy(prc[:, :, :], pr[:, bass.ds(c * CH, CH), :]).then_inc(rank_chain, 1)
                dve.wait_ge(rank_chain, c * 7 + 1)
                nc.vector.tensor_tensor(gt[:, :, :, :], other, mine, ALU.is_gt).then_inc(rank_chain, 1)
                nc.vector.tensor_tensor(eq[:, :, :, :], other, mine, ALU.is_equal).then_inc(rank_chain, 1)
                dve.wait_ge(rank_chain, c * 7 + 3)
                nc.vector.tensor_tensor(eq[:, :, :, :], eq[:, :, :, :], tri[:, :, :].unsqueeze(1).broadcast_to([P, CH, E, E]),
                                        ALU.mult).then_inc(rank_chain, 1)
                dve.wait_ge(rank_chain, c * 7 + 4)
                nc.vector.tensor_tensor(gt[:, :, :, :], gt[:, :, :, :], eq[:, :, :, :], ALU.add).then_inc(rank_chain, 1)
                dve.wait_ge(rank_chain, c * 7 + 5)
                nc.vector.tensor_reduce(rank[:, :, :], gt[:, :, :, :], AX.X, ALU.add).then_inc(rank_chain, 1)
                dve.wait_ge(rank_chain, c * 7 + 6)
                nc.vector.scalar_tensor_tensor(out=cwc[par][:, :, 1:E1], in0=rank[:, :, :], scalar=1.5, in1=prc[:, :, :],
                                               op0=ALU.is_lt, op1=ALU.mult).then_inc(rank_chain, 1)

            def start_sums(c):
                dve.wait_ge(acc_in, c + 1)
                dve.wait_ge(rank_chain, c * 7 + 7)

            def finish(c, par, stage):
                if stage == 0:
                    dve.wait_ge(acc_done, (c + 1) * SUMS)
                if stage < LN_STAGES:
                    normalise_rows(nc, dve, ln_chain, c * LN_STEPS(CH), acc[par], CH, lnst, lnmv, lntmp, stage)
                    return
                for i in range(CH):
                    nc.vector.tensor_scalar(acc[par][:, i, :], acc[par][:, i, :], lnmv[:, i, 0:1],
                                            lntmp[:, 1, i:i + 1], ALU.subtract, ALU.mult).then_inc(fin_done, 1)

            def last_normalise():
                dve.wait_ge(last_back, 48)
                nc.vector.tensor_tensor(last.ysum[:, :], last.yT1[:, :], last.yT2[:, :], ALU.add).then_inc(last_chain, 1)
                nc.vector.reciprocal(last.rden[:, :], last.den[:, :]).then_inc(last_chain, 1)
                dve.wait_ge(last_chain, 2)
                nc.vector.tensor_tensor(last.yT[:, :], last.ysum[:, :], last.rden[:, :], ALU.mult).then_inc(last_y, 1)

            def last_layer_norm():
                dve.wait_ge(last_proj, 1)
                nc.vector.tensor_tensor(last.rt[:, :, :], MX[:, 0:2 * C].rearrange("p (i c) -> p i c", i=2),
                                        last.xpb[:, :, :], ALU.add).then_inc(last_r, 1)
                dve.wait_ge(last_r, 1)
                for stage in range(LN_STAGES):
                    normalise_rows(nc, dve, last_ln, 0, last.rt, 2, last.lnst, last.lnmv, last.lntmp, stage)
                for i in range(2):
                    nc.vector.tensor_scalar(last.rt[:, i, :], last.rt[:, i, :], last.lnmv[:, i, 0:1],
                                            last.lntmp[:, 1, i:i + 1], ALU.subtract, ALU.mult).then_inc(last_x1, 1)

            def last_rows():
                dve.wait_ge(last_x1, 2)
                nc.vector.tensor_copy(R[:, NL:TILES, :], last.rt[:, :, :]).then_inc(last_chain, 1)
                dve.wait_ge(last_xh, 1)
                nc.vector.tensor_tensor(xTl[:, P * NL:P * NL + T], MX[:, 0:T], xTh[:, P * NL:P * NL + T],
                                        ALU.subtract).then_inc(last_xl, 1)
                dve.wait_ge(last_chain, 3)

            def add_bias(t0, t1):
                nc.vector.tensor_tensor(logit[:, t0:t1, :], LG[:, E * t0:E * t1].rearrange("p (t e) -> p t e", e=E),
                                        rb_bc[:, :].unsqueeze(1).broadcast_to([P, t1 - t0, E]), ALU.add).then_inc(logit_done, 1)

            def chunk(c, par, first=False, second=False):
                for e in range(E1):
                    hidden(c, 2 * e, first)
                    if e >= 2:
                        add(c, e - 2, par)
                    elif not first:
                        add(c, e - 2, 1 - par)
                    hidden(c, 2 * e + 1, first)
                    if e == 0:
                        begin(c, par)
                        if first:
                            weights_lo(0)
                        if second:
                            dve.wait_ge(logit_ready, 2)
                            add_bias(CH, TILES)
                    if e == 1:
                        rank_experts(c, par)
                        start_sums(c)
                        if first:
                            weights_lo(1)
                    if 2 <= e <= 2 + LN_STAGES and not first:
                        finish(c - 1, 1 - par, e - 2)
                    if first and e == 3:
                        last_normalise()
                    if first and e == 5:
                        last_layer_norm()
                    if first and e == 8:
                        last_rows()

            for par in range(2):
                nc.vector.memset(cwc[par][:, :, 0:1], 1.0).then_inc(ones_done, 1)
            dve.wait_ge(ones_done, 2)
            dve.wait_ge(logit_ready, 1)
            add_bias(0, CH)
            chunk(0, 0, first=True)
            chunk(1, 1, second=True)
            with dve.Fori(1, NCH // 2, 1) as i:
                chunk(i * 2, 0)
                chunk(i * 2 + 1, 1)
            add(NCH, -2, 1)
            add(NCH, -1, 1)
            for stage in range(LN_STAGES + 1):
                finish(NCH - 1, 1, stage)


def kernel(L0_attn_x, L0_attn_Wattn, L0_attn_battn, L0_attn_Wproj, L0_attn_bproj, L0_attn_embk,
           L0_attn_embv, L0_ffn_Wg_s, L0_ffn_Wu_s, L0_ffn_Wd_s, L0_ffn_Wg, L0_ffn_Wu, L0_ffn_Wd,
           L0_ffn_Wr, L0_ffn_rb):
    import ml_dtypes
    import numpy as np
    import concourse.bacc as bacc
    from concourse.bass_utils import run_bass_kernel_spmd

    f = lambda a: np.ascontiguousarray(np.asarray(a))
    x = f(L0_attn_x)
    B, T, C = x.shape
    E = L0_ffn_Wr.shape[0]
    bqkv = f(L0_attn_battn)
    last = L0_attn_embk.shape[0] - 1
    p = np.arange(128)
    dist = np.clip((p[:64, None] // 8) + T - 8 - np.arange(T + 8), 0, last)
    ekrows = np.tile(f(L0_attn_embk)[dist, p[:64, None] % 8], (2, 1))
    b, j, r = np.meshgrid(np.arange(2), np.arange(16), np.arange(8), indexing="ij")
    dist = np.clip(T - 1 - p[:, None] - (128 * b + 16 * r + j).reshape(1, -1), 0, last)
    evrows = f(L0_attn_embv)[dist].reshape(128, -1)
    gates = np.concatenate([f(L0_ffn_Wg_s)[None], f(L0_ffn_Wg)], 0)
    ups = np.concatenate([f(L0_ffn_Wu_s)[None], f(L0_ffn_Wu)], 0)
    downs = np.concatenate([f(L0_ffn_Wd_s)[None], f(L0_ffn_Wd)], 0)
    wup = np.stack([gates, ups], 0).transpose(3, 0, 1, 2)
    wdn = downs.reshape(E + 1, C, -1, 128).transpose(3, 0, 2, 1)
    m8 = (p[None, :] % 8 == (p[:, None] // 8) % 8).astype(np.float16)
    mh = (p[None, :] // 8 == p[:, None] // 8).astype(np.float16)
    sel8 = (p[:, None] == p[None, :] % 8).astype(ml_dtypes.bfloat16)
    u = np.arange(24) - 8
    causal = np.where((u[None, :] > p[:, None]) & (p[:, None] < 8), -1e30, 0.0).astype(ml_dtypes.bfloat16)
    tri = np.broadcast_to(np.tril(np.ones((E, E), np.float32), -1).reshape(1, -1), (128, E * E))
    arrays = {
        "x": x, "xT": f(x.reshape(B * T, C).T), "Wqkv": f(L0_attn_Wattn),
        "bqk": f(bqkv[0:2 * C].reshape(2, C).T), "bv": f(bqkv[2 * C:]),
        "Wp": f(L0_attn_Wproj), "bp": f(L0_attn_bproj),
        "ekrows": f(ekrows), "evrows": f(evrows),
        "Wup": f(wup), "Wdn": f(wdn), "WrT": f(f(L0_ffn_Wr).T), "rb": f(L0_ffn_rb),
        "ident": np.eye(128, dtype=np.float32), "m8": m8, "mh": mh, "sel8": f(sel8), "causal": causal, "tri": f(tri),
    }
    nc = bacc.Bacc("TRN2", target_bir_lowering=False, num_devices=1)
    args = [nc.dram_tensor(f"in_{k}", a.shape, mybir.dt.from_np(a.dtype), kind="ExternalInput").ap()
            for k, a in arrays.items()]
    out = nc.dram_tensor("out_0", x.shape, F32, kind="ExternalOutput").ap()
    attention_and_experts(nc, *args, out)
    r = run_bass_kernel_spmd(nc, [{f"in_{k}": a for k, a in arrays.items()}], core_ids=[0])
    return r.results[0]["out_0"]
```
